# Optimizing a Trainium2 kernel written in Bass

```python
import numpy as np
import jax
import jax.numpy as jnp

def _softmax(x, axis=-1):
    return jax.nn.softmax(x, axis=axis)

def _gelu(x):
    return jax.nn.gelu(x, approximate=True)

def _silu(x):
    return jax.nn.silu(x)

def _sigmoid(x):
    return jax.nn.sigmoid(x)

def _layernorm(x, axis=-1, eps=1e-05):
    m = jnp.mean(x, axis=axis, keepdims=True)
    v = jnp.var(x, axis=axis, keepdims=True)
    return (x - m) / jnp.sqrt(v + eps)

def _scatter_add(tgt, idx, src, axis=0):
    return tgt.at[idx].add(src)

def _segment_sum(src, seg, n):
    return jax.ops.segment_sum(src, seg, n)
kernel_name = 'mk_hybrid_d1_jaxref_r8_379b2b'

def setup_inputs(seed: int=0):
    np.random.seed(seed)
    _w = jnp.asarray

    def _L0_attn_a_setup():
        import jax, jax.numpy as jnp
        import numpy as np
        B, N, D = (4, 256, 128)
        H = 16
        HD = D // H
        SCALE = 1.0 / HD
        NEG = -10000.0
        THETA = 10000.0

        def _rope(t):
            d, n = (t.shape[-1], t.shape[-2])
            inv_freq = 1.0 / THETA ** (jnp.arange(0, d, 2, dtype=jnp.float32) / d)
            ang = jnp.arange(n, dtype=jnp.float32)[:, None] * inv_freq[None, :]
            cos = jnp.repeat(jnp.cos(ang), 2, axis=-1)
            sin = jnp.repeat(jnp.sin(ang), 2, axis=-1)
            x1, x2 = (t[..., ::2], t[..., 1::2])
            rot = jnp.stack([-x2, x1], axis=-1).reshape(t.shape)
            return t * cos + rot * sin
        key = jax.random.key(seed)
        ks = jax.random.split(key, 6)
        s = (1.0 / D) ** 0.5
        return {'x': jax.random.normal(ks[0], (B, N, D), jnp.float32), 'Wq': jax.random.normal(ks[1], (D, D), jnp.float32) * s, 'Wk': jax.random.normal(ks[2], (D, D), jnp.float32) * s, 'Wv': jax.random.normal(ks[3], (D, D), jnp.float32) * s, 'Wo': jax.random.normal(ks[4], (D, D), jnp.float32) * s, 'bo': jnp.zeros((D,), jnp.float32)}
    _L0_attn_a_in = _L0_attn_a_setup()

    def _L0_attn_b_setup():
        import jax, jax.numpy as jnp
        import numpy as np
        DIM = 128
        ED = 256
        N = 16
        K = 3
        B_SZ = 4
        L = 512
        key = jax.random.key(seed)
        ks = jax.random.split(key, 9)
        return {'x': jax.random.normal(ks[0], (B_SZ, L, DIM), jnp.float32), 'A': -jnp.exp(jax.random.normal(ks[1], (ED, N), jnp.float32)), 'Bm': jax.random.normal(ks[2], (ED, N), jnp.float32), 'Cm': jax.random.normal(ks[3], (N, ED), jnp.float32), 'Dv': jnp.ones((ED,), jnp.float32), 'W_dt': jax.random.normal(ks[4], (ED, 1), jnp.float32) * 0.02, 'conv_w': jax.random.normal(ks[5], (ED, 1, K), jnp.float32) * 0.1, 'W_in': jax.random.normal(ks[6], (2 * ED, DIM), jnp.float32) * (1.0 / np.sqrt(DIM)), 'W_out': jax.random.normal(ks[7], (DIM, ED), jnp.float32) * (1.0 / np.sqrt(ED))}
    _L0_attn_b_in = _L0_attn_b_setup()

    def _L0_ffn_setup():
        import jax, jax.numpy as jnp
        import numpy as np
        B, S, D, E, TOP_K = (2, 128, 128, 8, 2)
        H = 4 * D
        key = jax.random.key(seed)
        ks = jax.random.split(key, 12)
        sc = 0.02
        return {'x': jax.random.normal(ks[0], (B, S, D), jnp.float32), 'Wg': jax.random.normal(ks[1], (E, D), jnp.float32) * sc, 'bg': jnp.zeros((E,), jnp.float32), 'bias': jnp.zeros((E,), jnp.float32), 'W1': jax.random.normal(ks[2], (E, H, D), jnp.float32) * sc, 'b1': jnp.zeros((E, H), jnp.float32), 'W2': jax.random.normal(ks[3], (E, D, H), jnp.float32) * sc, 'b2': jnp.zeros((E, D), jnp.float32), 'Ws1': jax.random.normal(ks[4], (H, D), jnp.float32) * sc, 'bs1': jnp.zeros((H,), jnp.float32), 'Ws2': jax.random.normal(ks[5], (D, H), jnp.float32) * sc, 'bs2': jnp.zeros((D,), jnp.float32)}
    _L0_ffn_in = _L0_ffn_setup()
    _d = {'L0_attn_a_x': _L0_attn_a_in['x'], 'L0_attn_a_Wq': _L0_attn_a_in['Wq'], 'L0_attn_a_Wk': _L0_attn_a_in['Wk'], 'L0_attn_a_Wv': _L0_attn_a_in['Wv'], 'L0_attn_a_Wo': _L0_attn_a_in['Wo'], 'L0_attn_a_bo': _L0_attn_a_in['bo'], 'L0_attn_b_A': _L0_attn_b_in['A'], 'L0_attn_b_Bm': _L0_attn_b_in['Bm'], 'L0_attn_b_Cm': _L0_attn_b_in['Cm'], 'L0_attn_b_Dv': _L0_attn_b_in['Dv'], 'L0_attn_b_W_dt': _L0_attn_b_in['W_dt'], 'L0_attn_b_conv_w': _L0_attn_b_in['conv_w'], 'L0_attn_b_W_in': _L0_attn_b_in['W_in'], 'L0_attn_b_W_out': _L0_attn_b_in['W_out'], 'L0_ffn_Wg': _L0_ffn_in['Wg'], 'L0_ffn_bg': _L0_ffn_in['bg'], 'L0_ffn_bias': _L0_ffn_in['bias'], 'L0_ffn_W1': _L0_ffn_in['W1'], 'L0_ffn_b1': _L0_ffn_in['b1'], 'L0_ffn_W2': _L0_ffn_in['W2'], 'L0_ffn_b2': _L0_ffn_in['b2'], 'L0_ffn_Ws1': _L0_ffn_in['Ws1'], 'L0_ffn_bs1': _L0_ffn_in['bs1'], 'L0_ffn_Ws2': _L0_ffn_in['Ws2'], 'L0_ffn_bs2': _L0_ffn_in['bs2']}
    _x0 = _d['L0_attn_a_x']
    _d['L0_attn_a_x'] = jax.random.normal(jax.random.fold_in(jax.random.key(seed), 1), (4, 512, 128), dtype=_x0.dtype)
    del _x0
    return _d

def reference(L0_attn_a_x, L0_attn_a_Wq, L0_attn_a_Wk, L0_attn_a_Wv, L0_attn_a_Wo, L0_attn_a_bo, L0_attn_b_A, L0_attn_b_Bm, L0_attn_b_Cm, L0_attn_b_Dv, L0_attn_b_W_dt, L0_attn_b_conv_w, L0_attn_b_W_in, L0_attn_b_W_out, L0_ffn_Wg, L0_ffn_bg, L0_ffn_bias, L0_ffn_W1, L0_ffn_b1, L0_ffn_W2, L0_ffn_b2, L0_ffn_Ws1, L0_ffn_bs1, L0_ffn_Ws2, L0_ffn_bs2):

    def _L0_attn_a_ref(x, Wq, Wk, Wv, Wo, bo):
        import jax, jax.numpy as jnp
        import numpy as np
        B, N, D = (4, 256, 128)
        H = 16
        HD = D // H
        SCALE = 1.0 / HD
        NEG = -10000.0
        THETA = 10000.0

        def _rope(t):
            d, n = (t.shape[-1], t.shape[-2])
            inv_freq = 1.0 / THETA ** (jnp.arange(0, d, 2, dtype=jnp.float32) / d)
            ang = jnp.arange(n, dtype=jnp.float32)[:, None] * inv_freq[None, :]
            cos = jnp.repeat(jnp.cos(ang), 2, axis=-1)
            sin = jnp.repeat(jnp.sin(ang), 2, axis=-1)
            x1, x2 = (t[..., ::2], t[..., 1::2])
            rot = jnp.stack([-x2, x1], axis=-1).reshape(t.shape)
            return t * cos + rot * sin
        b, n, _ = x.shape
        q = (x @ Wq.T).reshape(b, n, H, HD).transpose(0, 2, 1, 3)
        k = (x @ Wk.T).reshape(b, n, H, HD).transpose(0, 2, 1, 3)
        v = (x @ Wv.T).reshape(b, n, H, HD).transpose(0, 2, 1, 3)
        q = _rope(q)
        k = _rope(k)
        i = jnp.arange(n)
        add_mask = jnp.where(i[:, None] >= i[None, :], 0.0, NEG).astype(x.dtype)
        scores = jnp.einsum('bhqd,bhkd->bhqk', q, k) * SCALE + add_mask
        attn = jax.nn.softmax(scores, axis=-1)
        out = jnp.einsum('bhqk,bhkd->bhqd', attn, v)
        out = out.transpose(0, 2, 1, 3).reshape(b, n, H * HD)
        return out @ Wo.T + bo

    def _L0_attn_b_ref(x, A, Bm, Cm, Dv, W_dt, conv_w, W_in, W_out):
        import jax, jax.numpy as jnp
        import numpy as np
        DIM = 128
        ED = 256
        N = 16
        K = 3
        B_SZ = 4
        L = 512
        residual = x
        proj = jnp.einsum('bld,ed->ble', x, W_in)
        x_conv, x_ssm = jnp.split(proj, 2, axis=-1)
        xc = jnp.transpose(x_conv, (0, 2, 1))
        xc = jax.lax.conv_general_dilated(xc, conv_w, window_strides=(1,), padding=[(K // 2, K // 2)], feature_group_count=ED, dimension_numbers=('NCH', 'OIH', 'NCH'))
        x_conv = jnp.transpose(xc, (0, 2, 1))
        dt = jax.lax.stop_gradient(jnp.mean(x_ssm, axis=-1))
        dtv = dt[..., None] * W_dt[:, 0]
        a = jnp.einsum('ble,en->bln', dtv, A)
        u = jnp.einsum('ble,en->bln', dtv * x_ssm, Bm)

        def step(m, au):
            a_t, u_t = au
            m = a_t * m + u_t
            return (m, m)
        m0 = jnp.zeros((x.shape[0], N), x.dtype)
        _, m_seq = jax.lax.scan(step, m0, (jnp.transpose(a, (1, 0, 2)), jnp.transpose(u, (1, 0, 2))))
        m_seq = jnp.transpose(m_seq, (1, 0, 2))
        y = jnp.einsum('bln,ne->ble', m_seq, Cm) + Dv * x_ssm
        gate = jax.nn.sigmoid(y)
        z = x_conv * gate + y * (1.0 - gate)
        return jnp.einsum('ble,de->bld', z, W_out) + residual

    def _L0_ffn_ref(x, Wg, bg, bias, W1, b1, W2, b2, Ws1, bs1, Ws2, bs2):
        import jax, jax.numpy as jnp
        import numpy as np
        B, S, D, E, TOP_K = (2, 128, 128, 8, 2)
        H = 4 * D
        b, s, d = x.shape
        xf = x.reshape(-1, d)
        T = xf.shape[0]
        scores = jax.nn.sigmoid(xf @ Wg.T + bg + bias)
        top_scores, top_idx = jax.lax.top_k(scores, TOP_K)
        weights = jnp.zeros((T, E), scores.dtype)
        weights = weights.at[jnp.arange(T)[:, None], top_idx].add(top_scores)
        h = jax.nn.gelu(jnp.einsum('td,ehd->teh', xf, W1) + b1, approximate=False)
        eo = jnp.einsum('teh,edh->ted', h, W2) + b2
        combined = jnp.einsum('ted,te->td', eo, weights)
        shared = jax.nn.gelu(xf @ Ws1.T + bs1, approximate=False) @ Ws2.T + bs2
        return (shared + combined).reshape(b, s, d)
    x = L0_attn_a_x
    x = x + _L0_attn_a_ref(_layernorm(x, axis=-1), L0_attn_a_Wq, L0_attn_a_Wk, L0_attn_a_Wv, L0_attn_a_Wo, L0_attn_a_bo)
    x = x + _L0_ffn_ref(_layernorm(x, axis=-1), L0_ffn_Wg, L0_ffn_bg, L0_ffn_bias, L0_ffn_W1, L0_ffn_b1, L0_ffn_W2, L0_ffn_b2, L0_ffn_Ws1, L0_ffn_bs1, L0_ffn_Ws2, L0_ffn_bs2)
    x = x + _L0_attn_b_ref(_layernorm(x, axis=-1), L0_attn_b_A, L0_attn_b_Bm, L0_attn_b_Cm, L0_attn_b_Dv, L0_attn_b_W_dt, L0_attn_b_conv_w, L0_attn_b_W_in, L0_attn_b_W_out)
    x = x + _L0_ffn_ref(_layernorm(x, axis=-1), L0_ffn_Wg, L0_ffn_bg, L0_ffn_bias, L0_ffn_W1, L0_ffn_b1, L0_ffn_W2, L0_ffn_b2, L0_ffn_Ws1, L0_ffn_bs1, L0_ffn_Ws2, L0_ffn_bs2)
    return x

_drawn_inputs = setup_inputs


def setup_inputs(seed=0):
    import zlib

    import numpy as np

    out = dict(_drawn_inputs(seed))
    spreads = {'L0_attn_a_bo': (0.0, 0.1),
     'L0_attn_b_Dv': (1.0, 0.2),
     'L0_ffn_bg': (0.0, 0.1),
     'L0_ffn_bias': (0.0, 0.1),
     'L0_ffn_b1': (0.0, 0.3),
     'L0_ffn_b2': (0.0, 0.1),
     'L0_ffn_bs1': (0.0, 0.1),
     'L0_ffn_bs2': (0.0, 0.1)}
    factors = {'L0_attn_b_A': 8.0}
    for name, (base, spread) in spreads.items():
        noise = np.random.default_rng([zlib.crc32(name.encode()), seed]).standard_normal(out[name].shape)
        drawn = base * np.exp(spread * noise) if base else spread * noise
        out[name] = jnp.asarray(drawn.astype(out[name].dtype))
    for name, factor in factors.items():
        out[name] = (out[name] * factor).astype(out[name].dtype)
    return out
```

```python
from contextlib import ExitStack

import numpy as np
import concourse.bass as bass
from concourse import mybir

ALU = mybir.AluOpType
ACT = mybir.ActivationFunctionType
AX = mybir.AxisListType
F32 = mybir.dt.float32
BF16 = mybir.dt.bfloat16

P = 128
D = 128
B = 4
L = 512
TT = L // P
H = 16
HD = D // H
G = 4
Q = 4
W = 32
E = 8
X = E + 1
F = 512
C = F // P
N = 16
ED = 256
K = 3
EPS = 1e-5
NEG_ROOT = 100.0
LNS = 4
FFNS = 2
S_UNITS = G * TT * Q
T_UNITS = G * TT * 2
ORDER = [E] + list(range(E))
DVE_LINKS = 52
GATE_PAD = 16


def hybrid_block_kernel(nc, x_in, wqkv_in, wo_in, bo_in, w1_in, b1_in, w2_in, b2_in, wg_in, bg_in, bias_in,
                        a_in, bm_in, cm_in, dv_in, wdt_in, conv_in, win_in, wout_in,
                        cos_in, sin_in, ident_in, neg_eye_in, mask_qk_in, mask_kq_in, pick_in, out):
    with ExitStack() as ctx:
        def sb(name, shape, dt=F32):
            return ctx.enter_context(nc.sbuf_tensor(name, shape, dt))

        def sem(name):
            return ctx.enter_context(nc.semaphore(name))

        ps = ctx.enter_context(nc.psum_tensor("ps", [P, 8, 512], F32))

        wqkv = sb("wqkv", [P, 3 * D])
        wo = sb("wo", [P, D])
        bo = sb("bo", [1, D])
        w1 = sb("w1", [P, X, F])
        b1 = sb("b1", [P, X * C])
        w2 = sb("w2", [P, X, C, D])
        b2 = sb("b2", [P, X])
        wg = sb("wg", [P, E])
        gate_rows = sb("gate_rows", [1, 2, E])
        a_mat = sb("a_mat", [P, 2, N])
        bm = sb("bm", [P, 2, N])
        cm = sb("cm", [N, ED])
        dv = sb("dv", [P, 2])
        wdt = sb("wdt", [P, 2])
        conv = sb("conv", [P, 2, K])
        win = sb("win", [P, 2 * ED])
        wout = sb("wout", [P, 2, D])
        cos = sb("cos", [P, TT, 2 * D])
        sin = sb("sin", [P, TT, 2 * D])
        ident = sb("ident", [P, P])
        ident16 = sb("ident16", [P, P], BF16)
        neg_eye = sb("neg_eye", [P, P], BF16)
        mask_qk = sb("mask_qk", [P, P], BF16)
        mask_kq = sb("mask_kq", [P, P], BF16)
        pick = sb("pick", [3 * E, E, P], BF16)
        ones = sb("ones", [1, P])
        mean_w = sb("mean_w", [P, N])
        minus_half = sb("minus_half", [P, TT])
        wb_mat = sb("wb_mat", [P, 2, N])
        wa = sb("wa", [N, 1])

        xin = sb("xin", [P, TT, D])
        x = sb("x", [P, TT, D])
        xout = sb("xout", [P, TT, D])
        stats = sb("stats", [P, TT, 6])
        mean_sum = sb("mean_sum", [P, TT])
        mean_dif = sb("mean_dif", [P, TT])
        sq_sum = sb("sq_sum", [P, TT])
        mean = sb("mean", [P, TT])
        spacer = sb("spacer", [P, 1])
        var_eps = sb("var_eps", [P, TT])
        rstd = sb("rstd", [P, TT])
        xn = sb("xn", [P, TT, D])
        xnT = sb("xnT", [P, L])

        rope_c = sb("rope_c", [P, TT, 2 * D])
        rope_s = sb("rope_s", [P, TT, 2 * D])
        qk_tok = sb("qk_tok", [P, TT, 2, H, W])
        v_tok = sb("v_tok", [P, TT, H, W])
        kT = sb("kT", [P, G, L])
        q1T = sb("q1T", [P, G, L])
        q2T = sb("q2T", [P, G, L])
        probs = sb("probs", [P, 3, 2, L])
        oT = sb("oT", [P, G, L])
        rec = sb("rec", [P, TT, H])
        att = sb("att", [P, TT, D])
        attT = sb("attT", [P, L])

        score = sb("score", [P, TT, GATE_PAD])
        best = sb("best", [P, TT, 8])
        taken = sb("taken", [P, TT, 8])
        left = sb("left", [P, TT, GATE_PAD])
        route = sb("route", [P, TT, E])
        rest = sb("rest", [P, TT, E])
        part = sb("part", [P, TT, 3 * E], BF16)
        partT = sb("partT", [3 * E, L], BF16)
        wide = sb("wide", [P, E, L])
        hid = sb("hid", [P, 2, C, L])
        tmp = sb("tmp", [P, 2, L])
        acc = sb("acc", [P, L])

        xs = sb("xs", [P, 2, L])
        xcv = sb("xcv", [P, 2, L])
        decay = sb("decay", [N, L])
        u_raw = sb("u_raw", [N, L])
        u_in = sb("u_in", [N, L])
        state = sb("state", [N, L])
        y, gate, diff, z = (wide[:, 2 * i:2 * i + 2, :] for i in range(4))

        consts_in = sem("consts_in")
        ffn_in = sem("ffn_in")
        scan_in = sem("scan_in")
        pads_set = sem("pads_set")
        dve_step = sem("dve_step")
        xin_ready = sem("xin_ready")
        xin_free = sem("xin_free")
        out_ready = sem("out_ready")
        out_stored = sem("out_stored")
        var_ready = sem("var_ready")
        rstd_ready = sem("rstd_ready")
        xn_ready = sem("xn_ready")
        xnT_made = sem("xnT_made")
        xnT_ready = sem("xnT_ready")
        v_made = sem("v_made")
        v_ready = sem("v_ready")
        qk_made = sem("qk_made")
        roped = sem("roped")
        kT_made = sem("kT_made")
        kT_ready = sem("kT_ready")
        q1T_made = sem("q1T_made")
        q1T_ready = sem("q1T_ready")
        score_made = sem("score_made")
        max_ready = sem("max_ready")
        q2T_made = sem("q2T_made")
        q2T_ready = sem("q2T_ready")
        st_made = sem("st_made")
        exp_ready = sem("exp_ready")
        pv_made = sem("pv_made")
        o_ready = sem("o_ready")
        otok_made = sem("otok_made")
        att_ready = sem("att_ready")
        attT_made = sem("attT_made")
        attT_ready = sem("attT_ready")
        wo_made = sem("wo_made")
        gate_made = sem("gate_made")
        sig_ready = sem("sig_ready")
        part_ready = sem("part_ready")
        partT_made = sem("partT_made")
        partT_ready = sem("partT_ready")
        wide_made = sem("wide_made")
        wide_ready = sem("wide_ready")
        up_made = sem("up_made")
        gelu_ready = sem("gelu_ready")
        down_made = sem("down_made")
        down_read = sem("down_read")
        acc_ready = sem("acc_ready")
        accT_made = sem("accT_made")
        wa_made = sem("wa_made")
        wa_ready = sem("wa_ready")
        wb_ready = sem("wb_ready")
        proj_made = sem("proj_made")
        xs_ready = sem("xs_ready")
        dtu_made = sem("dtu_made")
        u_ready = sem("u_ready")
        state_ready = sem("state_ready")
        y_made = sem("y_made")
        y_ready = sem("y_ready")
        gate_ready = sem("gate_ready")
        z_ready = sem("z_ready")
        mo_made = sem("mo_made")

        x_dram = x_in.rearrange("b (t p) d -> b p t d", p=P)
        out_dram = out.rearrange("b (t p) d -> b p t d", p=P)

        attn_loads = [(wqkv, wqkv_in), (cos, cos_in), (sin, sin_in), (ident, ident_in), (wo, wo_in), (bo, bo_in),
                      (neg_eye, neg_eye_in), (mask_qk, mask_qk_in), (mask_kq, mask_kq_in)]
        ffn_loads = [(wg, wg_in), (gate_rows[:, 0, :], bg_in), (gate_rows[:, 1, :], bias_in), (w1, w1_in),
                     (b1, b1_in), (w2, w2_in), (b2, b2_in), (pick, pick_in)]
        scan_loads = [(a_mat, a_in), (bm, bm_in), (cm, cm_in), (dv, dv_in), (wdt, wdt_in), (conv, conv_in),
                      (win, win_in), (wout, wout_in)]

        block = ctx.enter_context(nc.Block())

        def whole(t):
            return t[:] if not isinstance(t, bass.AP) else t

        @block.sync
        def _(sp):
            for dst, src in attn_loads[:4]:
                sp.dma_start(whole(dst), src).then_inc(consts_in, 16)
            sp.dma_start(xin[:], x_dram[0]).then_inc(xin_ready, 16)
            for dst, src in attn_loads[4:]:
                sp.dma_start(whole(dst), src).then_inc(consts_in, 16)
            for dst, src in ffn_loads:
                sp.dma_start(whole(dst), src).then_inc(ffn_in, 16)
            for dst, src in scan_loads:
                sp.dma_start(whole(dst), src).then_inc(scan_in, 16)
            with sp.Fori(1, B) as b:
                sp.wait_ge(xin_free, b)
                sp.dma_start(xin[:], x_dram[bass.ds(b, 1)].rearrange("o p t d -> (o p) t d")).then_inc(xin_ready, 16)

        @block.gpsimd
        def _(pool):
            nc.gpsimd.memset(minus_half[:], -0.5).then_inc(pads_set, 1)
            nc.gpsimd.memset(v_tok[:], 0.0)
            nc.gpsimd.memset(score[:], -1.0)
            nc.gpsimd.memset(taken[:], -1.0)
            nc.gpsimd.memset(ones[:], 1.0)
            nc.gpsimd.memset(mean_w[:], 1.0 / ED).then_inc(pads_set, 1)
            pool.wait_ge(pads_set, 2)
            nc.gpsimd.memset(v_tok[:, :, :, HD:HD + 1], 1.0).then_inc(pads_set, 1)
            with pool.Fori(0, B) as b:
                for r in range(LNS):
                    pool.wait_ge(var_ready, b * LNS + r + 1)
                    nc.gpsimd.tensor_tensor(rstd[:], var_eps[:], minus_half[:], ALU.pow).then_inc(rstd_ready, 1)

        @block.scalar
        def _(act):
            def norm_T(b, r):
                act.wait_ge(xnT_made, b * LNS + r + 1)
                nc.scalar.copy(xnT[:], ps[:, 0, :]).then_inc(xnT_ready, 1)

            def attention(b):
                norm_T(b, 0)
                act.wait_ge(v_made, b + 1)
                act.wait_ge(pads_set, 3)
                nc.scalar.copy(v_tok[:, :, :, 0:HD],
                               ps[:, 1, :].rearrange("p (t h d) -> p t h d", t=TT, h=H)).then_inc(v_ready, 1)
                for g in range(G):
                    act.wait_ge(kT_made, b * G + g + 1)
                    nc.scalar.copy(kT[:, g, :], ps[:, g, :]).then_inc(kT_ready, 1)
                for g in range(G):
                    act.wait_ge(q2T_made, b * G + g + 1)
                    nc.scalar.copy(q2T[:, g, :], ps[:, 7, :]).then_inc(q2T_ready, 1)
                    for j in range(TT):
                        for pr in range(2):
                            m = (g * TT + j) * 2 + pr
                            n = L - P * j
                            bank = 2 + 2 * (m % 2)
                            act.wait_ge(st_made, b * T_UNITS + m + 1)
                            if m >= 3:
                                act.wait_ge(pv_made, b * T_UNITS + m - 2)
                            nc.scalar.activation(probs[:, m % 3, :, 0:n], ps[:, bank:bank + 2, 0:n],
                                                 ACT.Exp).then_inc(exp_ready, 1)
                act.wait_ge(attT_made, b + 1)
                nc.scalar.copy(attT[:], ps[:, 4, :]).then_inc(attT_ready, 1)

            def ffn(b, r):
                f = b * FFNS + r
                norm_T(b, 1 + 2 * r)
                act.wait_ge(gate_made, f + 1)
                act.wait_ge(pads_set, 3)
                nc.scalar.activation(score[:, :, 0:E], ps[:, 1, 0:TT * E].rearrange("p (t e) -> p t e", t=TT),
                                     ACT.Sigmoid).then_inc(sig_ready, 1)

                def wide_copy(e):
                    act.wait_ge(wide_made, f * E + e + 1)
                    nc.scalar.copy(wide[:, e, :], ps[:, 2 + e % 2, :]).then_inc(wide_ready, 1)

                for i in range(X):
                    for c in range(C):
                        n = i * C + c
                        act.wait_ge(up_made, f * X * C + n + 1)
                        if i >= 2 and c == 0:
                            act.wait_ge(down_made, f * X + i - 1)
                        nc.scalar.activation(hid[:, i % 2, c, :], ps[:, 4 + n % 2, :], ACT.Gelu,
                                             bias=b1[:, ORDER[i] * C + c:ORDER[i] * C + c + 1]).then_inc(gelu_ready, 1)
                    if i == 1:
                        act.wait_ge(partT_made, f + 1)
                        nc.scalar.copy(partT[:], ps[0:3 * E, 0, 0:L // 2].bitcast(BF16)).then_inc(partT_ready, 1)
                    if i == 2:
                        wide_copy(0)
                        wide_copy(1)
                    if i >= 3:
                        wide_copy(i - 1)

            def scan_block(b):
                norm_T(b, 2)
                for c in range(2):
                    act.wait_ge(proj_made, b * 4 + c + 1)
                    nc.scalar.copy(xs[:, c, :], ps[:, 3 + c, :]).then_inc(xs_ready, 1)
                act.wait_ge(dtu_made, b + 1)
                nc.scalar.copy(u_raw[:], ps[0:N, 6, :]).then_inc(u_ready, 1)
                act.wait_ge(y_ready, b + 1)
                nc.scalar.activation(gate, y, ACT.Sigmoid).then_inc(gate_ready, 1)

            act.wait_ge(ffn_in, 16 * len(ffn_loads))
            act.wait_ge(wa_made, 1)
            nc.scalar.copy(wa[:], ps[0:N, 7, 0:1]).then_inc(wa_ready, 1)
            with act.Fori(0, B) as b:
                attention(b)
                ffn(b, 0)
                scan_block(b)
                ffn(b, 1)
                act.wait_ge(out_ready, b + 1)
                act.dma_start(out_dram[bass.ds(b, 1)].rearrange("o p t d -> (o p) t d"),
                              xout[:]).then_inc(out_stored, 16)
            act.wait_ge(out_stored, 16 * B)

        @block.tensor
        def _(pe):
            def norm_T(b, r):
                pe.wait_ge(xn_ready, b * LNS + r + 1)
                for t in range(TT):
                    mm = pe.transpose(ps[:, 0, t * P:(t + 1) * P], xn[:, t, :], ident[:])
                mm.then_inc(xnT_made, 1)
                pe.wait_ge(xnT_ready, b * LNS + r + 1)

            def scores(b, g, t, q):
                n = (g * TT + t) * Q + q
                keys = P * (t + 1)
                if n >= 2:
                    pe.wait_ge(max_ready, b * S_UNITS + n - 1)
                pe.matmul(ps[:, n % 2, 0:keys], q1T[W * q:W * q + HD, g, t * P:(t + 1) * P],
                          kT[W * q:W * q + HD, g, 0:keys], start=True, stop=False)
                pe.matmul(ps[:, n % 2, keys - P:keys], neg_eye[:], mask_qk[:],
                          start=False, stop=True).then_inc(score_made, 1)

            def queries_with_max(b, g):
                pe.wait_ge(max_ready, b * S_UNITS + TT * Q * (g + 1))
                for t in range(TT):
                    mm = pe.transpose(ps[:, 7, t * P:(t + 1) * P],
                                      qk_tok[:, t, 0, Q * g:Q * g + Q, :].rearrange("p h w -> p (h w)"), ident[:])
                mm.then_inc(q2T_made, 1)

            def scores_T(b, m):
                g, j, pr = m // (2 * TT), m // 2 % TT, m % 2
                n = L - P * j
                bank = 2 + 2 * (m % 2)
                if m % (2 * TT) == 0:
                    pe.wait_ge(q2T_ready, b * G + g + 1)
                if m >= 2:
                    pe.wait_ge(exp_ready, b * T_UNITS + m - 1)
                for h in range(2):
                    r = W * (2 * pr + h)
                    pe.matmul(ps[:, bank + h, 0:n], kT[r:r + HD + 1, g, j * P:(j + 1) * P],
                              q2T[r:r + HD + 1, g, j * P:L], start=True, stop=False)
                for h in range(2):
                    mm = pe.matmul(ps[:, bank + h, 0:P], neg_eye[:], mask_kq[:], start=False, stop=True)
                mm.then_inc(st_made, 1)

            def weigh_values(b, m):
                g, j, pr = m // (2 * TT), m // 2 % TT, m % 2
                n = L - P * j
                if m % (2 * TT) == 0:
                    pe.wait_ge(o_ready, b * G + g)
                pe.wait_ge(exp_ready, b * T_UNITS + m + 1)
                for h in range(2):
                    r = 2 * pr + h
                    mm = pe.matmul(ps[W * r:W * r + W, 6, j * P:L], v_tok[:, j, Q * g + r, :],
                                   probs[:, m % 3, h, 0:n], start=(j == 0), stop=(j == TT - 1))
                mm.then_inc(pv_made, 1)

            def attention(b):
                norm_T(b, 0)
                for t in range(TT):
                    pe.matmul(ps[:, 4 + t, 0:2 * D], xnT[:, t * P:(t + 1) * P], wqkv[:, 0:2 * D],
                              start=True, stop=True).then_inc(qk_made, 1)
                for t in range(TT):
                    mm = pe.matmul(ps[:, 1, t * D:(t + 1) * D], xnT[:, t * P:(t + 1) * P], wqkv[:, 2 * D:3 * D],
                                   start=True, stop=True)
                mm.then_inc(v_made, 1)
                pe.wait_ge(roped, b + 1)
                pe.wait_ge(v_ready, b + 1)
                for g in range(G):
                    for t in range(TT):
                        mm = pe.transpose(ps[:, g, t * P:(t + 1) * P],
                                          qk_tok[:, t, 1, Q * g:Q * g + Q, :].rearrange("p h w -> p (h w)"), ident[:])
                    mm.then_inc(kT_made, 1)
                    for t in range(TT):
                        mm = pe.transpose(ps[:, 4 + g, t * P:(t + 1) * P],
                                          qk_tok[:, t, 0, Q * g:Q * g + Q, :].rearrange("p h w -> p (h w)"), ident[:])
                    mm.then_inc(q1T_made, 1)
                pe.wait_ge(kT_ready, b * G + G)
                pe.wait_ge(q1T_ready, b * G + G)
                for u in range(TT * Q):
                    scores(b, 0, u // Q, u % Q)
                per = 2 * TT
                for g in range(G):
                    queries_with_max(b, g)
                    scores_T(b, g * per)
                    for i in range(per):
                        if g + 1 < G:
                            for u in (2 * i, 2 * i + 1):
                                scores(b, g + 1, u // Q, u % Q)
                        if i + 1 < per:
                            scores_T(b, g * per + i + 1)
                        weigh_values(b, g * per + i)
                pe.wait_ge(o_ready, b * G + G)
                for t in range(TT):
                    for g in range(G):
                        mm = pe.transpose(ps[:, t, g * P:(g + 1) * P], oT[:, g, t * P:(t + 1) * P], ident[:])
                    mm.then_inc(otok_made, 1)
                pe.wait_ge(att_ready, b + 1)
                for t in range(TT):
                    mm = pe.transpose(ps[:, 4, t * P:(t + 1) * P], att[:, t, :], ident[:])
                mm.then_inc(attT_made, 1)
                pe.wait_ge(attT_ready, b + 1)
                for t in range(TT):
                    pe.matmul(ps[:, 5, t * D:(t + 1) * D], attT[:, t * P:(t + 1) * P], wo[:], start=True, stop=False)
                    mm = pe.matmul(ps[:, 5, t * D:(t + 1) * D], ones[:], bo[:], start=False, stop=True)
                mm.then_inc(wo_made, 1)

            def ffn(b, r):
                f = b * FFNS + r
                norm_T(b, 1 + 2 * r)
                for t in range(TT):
                    o = ps[:, 1, t * E:(t + 1) * E]
                    pe.matmul(o, xnT[:, t * P:(t + 1) * P], wg[:], start=True, stop=False)
                    pe.matmul(o, ones[:], gate_rows[:, 0, :], start=False, stop=False)
                    mm = pe.matmul(o, ones[:], gate_rows[:, 1, :], start=False, stop=True)
                mm.then_inc(gate_made, 1)

                def up(i, c):
                    n = i * C + c
                    if n >= 2:
                        pe.wait_ge(gelu_ready, f * X * C + n - 1)
                    pe.matmul(ps[:, 4 + n % 2, :], w1[:, ORDER[i], c * P:(c + 1) * P], xnT[:],
                              start=True, stop=True).then_inc(up_made, 1)

                def down(i, c):
                    if c == 0 and i >= 2:
                        pe.wait_ge(down_read, f * X + i - 1)
                    pe.wait_ge(gelu_ready, f * X * C + i * C + c + 1)
                    mm = pe.matmul(ps[:, 6 + i % 2, :], w2[:, ORDER[i], c, :], hid[:, i % 2, c, :],
                                   start=(c == 0), stop=(c == C - 1))
                    if c == C - 1:
                        mm.then_inc(down_made, 1)

                def widen(e):
                    if e >= 2:
                        pe.wait_ge(wide_ready, f * E + e - 1)
                    pe.matmul(ps[:, 2 + e % 2, :], pick[:, e, :], partT[:], start=True,
                              stop=True).then_inc(wide_made, 1)

                for c in range(C):
                    up(0, c)
                for i in range(X):
                    for c in range(C):
                        if i + 1 < X:
                            up(i + 1, c)
                        down(i, c)
                    if i == 0:
                        pe.wait_ge(part_ready, f + 1)
                        for t in range(TT):
                            mm = pe.transpose(ps[0:3 * E, 0, t * (P // 2):(t + 1) * (P // 2)].bitcast(BF16),
                                              part[:, t, :], ident16[:])
                        mm.then_inc(partT_made, 1)
                    if i == 1:
                        pe.wait_ge(partT_ready, f + 1)
                        widen(0)
                        widen(1)
                    if 2 <= i < E:
                        widen(i)
                pe.wait_ge(acc_ready, f + 1)
                for t in range(TT):
                    mm = pe.transpose(ps[:, 1, t * P:(t + 1) * P], acc[:, t * P:(t + 1) * P], ident[:])
                mm.then_inc(accT_made, 1)

            def scan_block(b):
                norm_T(b, 2)
                for n, k in enumerate((2, 3, 0, 1)):
                    pe.matmul(ps[:, 1 + k, :], win[:, k * P:(k + 1) * P], xnT[:], start=True,
                              stop=True).then_inc(proj_made, 1)
                pe.wait_ge(xs_ready, b * 2 + 2)
                for c in range(2):
                    pe.matmul(ps[0:N, 6, :], wb_mat[:, c, :], xs[:, c, :], start=(c == 0), stop=(c == 1))
                for c in range(2):
                    mm = pe.matmul(ps[0:N, 5, :], mean_w[:], xs[:, c, :], start=(c == 0), stop=(c == 1))
                mm.then_inc(dtu_made, 1)
                pe.wait_ge(state_ready, b + 1)
                for c in range(2):
                    pe.matmul(ps[:, 7 * (1 - c), :], cm[:, c * P:(c + 1) * P], state[:], start=True,
                              stop=True).then_inc(y_made, 1)
                pe.wait_ge(z_ready, b + 1)
                for t in range(TT):
                    for c in range(2):
                        mm = pe.matmul(ps[:, 1, t * D:(t + 1) * D], z[:, c, t * P:(t + 1) * P], wout[:, c, :],
                                       start=(c == 0), stop=(c == 1))
                mm.then_inc(mo_made, 1)

            pe.wait_ge(scan_in, 16 * len(scan_loads))
            for c in range(2):
                mm = pe.matmul(ps[0:N, 7, 0:1], a_mat[:, c, :], wdt[:, c:c + 1], start=(c == 0), stop=(c == 1))
            mm.then_inc(wa_made, 1)
            pe.wait_ge(wa_ready, 1)
            pe.wait_ge(consts_in, 16 * len(attn_loads))
            pe.wait_ge(ffn_in, 16 * len(ffn_loads))
            pe.wait_ge(pads_set, 3)
            pe.wait_ge(wb_ready, 1)
            with pe.Fori(0, B) as b:
                attention(b)
                ffn(b, 0)
                scan_block(b)
                ffn(b, 1)

        @block.vector
        def _(dve):
            links = [0]

            def link(b, ins):
                links[0] += 1
                ins.then_inc(dve_step, 1)
                dve.wait_ge(dve_step, b * DVE_LINKS + links[0] + 4)

            def norm(b, r, src):
                for t in range(TT):
                    ins = nc.vector.bn_stats(stats[:, t, :], src[:, t, :])
                link(b, ins)
                mean_e, sq_e, mean_o, sq_o = (stats[:, :, i] for i in (1, 2, 4, 5))
                nc.vector.tensor_tensor(mean_sum[:], mean_e, mean_o, ALU.add)
                nc.vector.tensor_tensor(mean_dif[:], mean_e, mean_o, ALU.subtract)
                link(b, nc.vector.scalar_tensor_tensor(sq_sum[:], sq_e, D * EPS, sq_o, ALU.add, ALU.add))
                nc.vector.tensor_scalar(mean[:], mean_sum[:], 0.5, None, ALU.mult)
                link(b, nc.vector.scalar_tensor_tensor(mean_dif[:], mean_dif[:], 0.25, mean_dif[:], ALU.mult, ALU.mult))
                nc.vector.scalar_tensor_tensor(var_eps[:], sq_sum[:], 1.0 / D, mean_dif[:], ALU.mult,
                                               ALU.add).then_inc(var_ready, 1)
                dve.wait_ge(rstd_ready, b * LNS + r + 1)
                for t in range(TT):
                    ins = nc.vector.tensor_scalar(xn[:, t, :], src[:, t, :], mean[:, t:t + 1], rstd[:, t:t + 1],
                                                  ALU.subtract, ALU.mult)
                ins.then_inc(xn_ready, 1)

            def row_max(b, g):
                for t in range(TT):
                    for q in range(Q):
                        n = (g * TT + t) * Q + q
                        dve.wait_ge(score_made, b * S_UNITS + n + 1)
                        nc.vector.tensor_reduce(qk_tok[:, t, 0, Q * g + q, HD:HD + 1], ps[:, n % 2, 0:P * (t + 1)],
                                                AX.X, ALU.max).then_inc(max_ready, 1)

            def attention(b):
                dve.wait_ge(xin_ready, b * 16 + 16)
                norm(b, 0, xin)
                for t in range(TT):
                    dve.wait_ge(qk_made, b * TT + t + 1)
                    qk = ps[:, 4 + t, 0:2 * D]
                    turned = rope_s[:, t, :].rearrange("p (i two) -> p i two", two=2)
                    pairs = qk.rearrange("p (i two) -> p i two", two=2)
                    s = sin[:, t, :].rearrange("p (i two) -> p i two", two=2)
                    nc.vector.tensor_tensor(rope_c[:, t, :], qk, cos[:, t, :], ALU.mult)
                    nc.vector.tensor_tensor(turned[:, :, 0], pairs[:, :, 1], s[:, :, 0], ALU.mult)
                    ins = nc.vector.tensor_tensor(turned[:, :, 1], pairs[:, :, 0], s[:, :, 1], ALU.mult)
                link(b, ins)
                for t in range(TT):
                    ins = nc.vector.tensor_tensor(
                        qk_tok[:, t, :, :, 0:HD],
                        rope_c[:, t, :].rearrange("p (k h d) -> p k h d", k=2, h=H),
                        rope_s[:, t, :].rearrange("p (k h d) -> p k h d", k=2, h=H), ALU.add)
                ins.then_inc(roped, 1)
                for g in range(G):
                    dve.wait_ge(q1T_made, b * G + g + 1)
                    nc.vector.tensor_copy(q1T[:, g, :], ps[:, 4 + g, :]).then_inc(q1T_ready, 1)
                row_max(b, 0)
                for g in range(G):
                    if g + 1 < G:
                        row_max(b, g + 1)
                    dve.wait_ge(pv_made, b * T_UNITS + 2 * TT * (g + 1))
                    nc.vector.tensor_copy(oT[:, g, :], ps[:, 6, :]).then_inc(o_ready, 1)
                for t in range(TT):
                    dve.wait_ge(otok_made, b * TT + t + 1)
                    ins = nc.vector.reciprocal(rec[:, t, :], ps[:, t, :].rearrange("p (h w) -> p h w", w=W)[:, :, HD])
                link(b, ins)
                for t in range(TT):
                    ins = nc.vector.tensor_tensor(
                        att[:, t, :].rearrange("p (h d) -> p h d", h=H),
                        ps[:, t, :].rearrange("p (h w) -> p h w", w=W)[:, :, 0:HD],
                        rec[:, t, :].unsqueeze(2).broadcast_to([P, H, HD]), ALU.mult)
                ins.then_inc(att_ready, 1)
                dve.wait_ge(wo_made, b + 1)
                ins = nc.vector.tensor_tensor(x[:].rearrange("p t d -> p (t d)"), ps[:, 5, :],
                                              xin[:].rearrange("p t d -> p (t d)"), ALU.add)
                link(b, ins)
                nc.vector.tensor_copy(rec[:, 0, 0:1], x[:, 0, 0:1]).then_inc(xin_free, 1)

            def ffn(b, r):
                f = b * FFNS + r
                norm(b, 1 + 2 * r, x)
                dve.wait_ge(sig_ready, f + 1)
                nc.vector.memset(spacer[:], 0.0)
                for t in range(TT):
                    ins = nc.vector.max(best[:, t, :], score[:, t, :])
                link(b, ins)
                link(b, nc.vector.tensor_copy(taken[:, :, 0:2], best[:, :, 0:2]))
                nc.vector.memset(spacer[:], 0.0)
                for t in range(TT):
                    ins = nc.vector.match_replace(left[:, t, :], taken[:, t, :], score[:, t, :], 0.0)
                link(b, ins)
                link(b, nc.vector.tensor_tensor(route[:], score[:, :, 0:E], left[:, :, 0:E], ALU.subtract))
                link(b, nc.vector.tensor_copy(part[:, :, 0:E], route[:]))
                link(b, nc.vector.tensor_tensor(rest[:], route[:], part[:, :, 0:E], ALU.subtract))
                link(b, nc.vector.tensor_copy(part[:, :, E:2 * E], rest[:]))
                link(b, nc.vector.tensor_tensor(route[:], rest[:], part[:, :, E:2 * E], ALU.subtract))
                nc.vector.tensor_copy(part[:, :, 2 * E:3 * E], route[:]).then_inc(part_ready, 1)
                for i in range(X):
                    e = ORDER[i]
                    dve.wait_ge(down_made, f * X + i + 1)
                    if i == 0:
                        nc.vector.tensor_scalar(acc[:], ps[:, 6, :], b2[:, e:e + 1], None,
                                                ALU.add).then_inc(down_read, 1)
                        continue
                    dve.wait_ge(wide_ready, f * E + e + 1)
                    nc.vector.scalar_tensor_tensor(tmp[:, i % 2, :], ps[:, 6 + i % 2, :], b2[:, e:e + 1],
                                                   wide[:, e, :], ALU.add, ALU.mult).then_inc(down_read, 1)
                    dve.wait_ge(down_read, f * X + i + 1)
                    ins = nc.vector.tensor_tensor(acc[:], acc[:], tmp[:, i % 2, :], ALU.add)
                    if i < E:
                        link(b, ins)
                    else:
                        ins.then_inc(acc_ready, 1)
                dve.wait_ge(accT_made, f + 1)
                x_flat = x[:].rearrange("p t d -> p (t d)")
                if r == 0:
                    link(b, nc.vector.tensor_tensor(x_flat, ps[:, 1, :], x_flat, ALU.add))
                else:
                    dve.wait_ge(out_stored, b * 16)
                    nc.vector.tensor_tensor(xout[:].rearrange("p t d -> p (t d)"), ps[:, 1, :], x_flat,
                                            ALU.add).then_inc(out_ready, 1)

            def scan_block(b):
                norm(b, 2, x)
                x_flat = x[:].rearrange("p t d -> p (t d)")
                dve.wait_ge(xn_ready, b * LNS + 3)
                nc.vector.tensor_tensor(x_flat, x_flat, xn[:].rearrange("p t d -> p (t d)"), ALU.add)
                dve.wait_ge(proj_made, b * 4 + 4)
                for c in range(2):
                    ins = nc.vector.tensor_scalar(xcv[:, c, :], ps[:, 1 + c, :], conv[:, c, 1:2], None, ALU.mult)
                link(b, ins)
                for c in range(2):
                    ins = nc.vector.scalar_tensor_tensor(xcv[:, c, 1:L], ps[:, 1 + c, 0:L - 1], conv[:, c, 0:1],
                                                         xcv[:, c, 1:L], ALU.mult, ALU.add)
                link(b, ins)
                for c in range(2):
                    ins = nc.vector.scalar_tensor_tensor(xcv[:, c, 0:L - 1], ps[:, 1 + c, 1:L], conv[:, c, 2:3],
                                                         xcv[:, c, 0:L - 1], ALU.mult, ALU.add)
                dve.wait_ge(dtu_made, b + 1)
                nc.vector.tensor_scalar(decay[:], ps[0:N, 5, :], wa[:, 0:1], None, ALU.mult)
                dve.wait_ge(u_ready, b + 1)
                link(b, nc.vector.tensor_tensor(u_in[:], u_raw[:], ps[0:N, 5, :], ALU.mult))
                nc.vector.tensor_tensor_scan(state[:], decay[:], u_in[:], 0.0, ALU.mult,
                                             ALU.add).then_inc(state_ready, 1)
                for c in range(2):
                    dve.wait_ge(y_made, b * 2 + c + 1)
                    ins = nc.vector.scalar_tensor_tensor(y[:, c, :], xs[:, c, :], dv[:, c:c + 1],
                                                         ps[:, 7 * (1 - c), :], ALU.mult, ALU.add)
                ins.then_inc(y_ready, 1)
                dve.wait_ge(y_ready, b + 1)
                link(b, nc.vector.tensor_tensor(diff, xcv[:], y, ALU.subtract))
                dve.wait_ge(gate_ready, b + 1)
                link(b, nc.vector.tensor_tensor(diff, diff, gate, ALU.mult))
                nc.vector.tensor_tensor(z, diff, y, ALU.add).then_inc(z_ready, 1)
                dve.wait_ge(mo_made, b + 1)
                link(b, nc.vector.tensor_tensor(x_flat, ps[:, 1, :], x_flat, ALU.add))

            nc.vector.memset(qk_tok[:], 0.0).then_inc(dve_step, 1)
            dve.wait_ge(dve_step, 1)
            nc.vector.memset(qk_tok[:, :, 1, :, HD:HD + 1], -1.0).then_inc(dve_step, 1)
            dve.wait_ge(consts_in, 16 * len(attn_loads))
            nc.vector.tensor_copy(ident16[:], ident[:]).then_inc(dve_step, 1)
            dve.wait_ge(scan_in, 16 * len(scan_loads))
            for c in range(2):
                ins = nc.vector.tensor_scalar(wb_mat[:, c, :], bm[:, c, :], wdt[:, c:c + 1], None, ALU.mult)
            ins.then_inc(dve_step, 1)
            dve.wait_ge(dve_step, 4)
            nc.vector.memset(rec[:, 0, 0:1], 0.0).then_inc(wb_ready, 1)
            dve.wait_ge(ffn_in, 16 * len(ffn_loads))
            dve.wait_ge(pads_set, 3)
            dve.wait_ge(wa_ready, 1)
            dve.wait_ge(wb_ready, 1)
            with dve.Fori(0, B) as b:
                links[0] = 0
                attention(b)
                ffn(b, 0)
                scan_block(b)
                ffn(b, 1)
                assert links[0] == DVE_LINKS, links[0]


def shape_constants():
    inv_freq = (1.0 / np.float32(10000.0) ** (np.arange(0, HD, 2, dtype=np.float32) / np.float32(HD))).astype(np.float32)
    ang = np.arange(L, dtype=np.float32)[:, None] * inv_freq[None, :]
    cos = np.repeat(np.cos(ang), 2, axis=-1)
    sin = np.repeat(np.sin(ang), 2, axis=-1) * np.where(np.arange(HD) % 2 == 0, -1.0, 1.0)
    scale = np.array([1.0 / HD, 1.0])[:, None, None]

    def table(a):
        a = np.broadcast_to(a.reshape(TT, P, 1, 1, HD), (TT, P, 2, H, HD)) * scale
        return np.ascontiguousarray(a.transpose(1, 0, 2, 3, 4).reshape(P, TT, 2 * D)).astype(np.float32)

    bf = mybir.dt.np(BF16)
    later = np.arange(P)[None, :] > np.arange(P)[:, None]
    pick = np.zeros((3, E, E, P), np.float32)
    for e in range(E):
        pick[:, e, e, :] = 1.0
    return {
        "cos": table(cos), "sin": table(sin), "ident": np.eye(P, dtype=np.float32),
        "neg_eye": (NEG_ROOT * np.eye(P)).astype(bf),
        "mask_qk": (-NEG_ROOT * later).astype(bf), "mask_kq": (-NEG_ROOT * later.T).astype(bf),
        "pick": pick.reshape(3 * E, E, P).astype(bf),
    }


def kernel(**inputs):
    import concourse.bacc as bacc
    from concourse.bass_utils import run_bass_kernel_spmd

    a = {k: np.asarray(v) for k, v in inputs.items()}
    w1 = np.concatenate([a["L0_ffn_W1"], a["L0_ffn_Ws1"][None]], 0)
    w2 = np.concatenate([a["L0_ffn_W2"], a["L0_ffn_Ws2"][None]], 0)
    b1 = np.concatenate([a["L0_ffn_b1"], a["L0_ffn_bs1"][None]], 0)
    b2 = np.concatenate([a["L0_ffn_b2"], a["L0_ffn_bs2"][None]], 0)
    arrays = {
        "x": a["L0_attn_a_x"],
        "wqkv": np.concatenate([a["L0_attn_a_Wq"].T, a["L0_attn_a_Wk"].T, a["L0_attn_a_Wv"].T], 1),
        "wo": a["L0_attn_a_Wo"].T,
        "bo": a["L0_attn_a_bo"][None],
        "w1": w1.transpose(2, 0, 1),
        "b1": b1.reshape(X * C, P).T,
        "w2": w2.reshape(X, D, C, P).transpose(3, 0, 2, 1),
        "b2": b2.T,
        "wg": a["L0_ffn_Wg"].T,
        "bg": a["L0_ffn_bg"][None],
        "bias": a["L0_ffn_bias"][None],
        "a_mat": a["L0_attn_b_A"].reshape(2, P, N).transpose(1, 0, 2),
        "bm": a["L0_attn_b_Bm"].reshape(2, P, N).transpose(1, 0, 2),
        "cm": a["L0_attn_b_Cm"],
        "dv": a["L0_attn_b_Dv"].reshape(2, P).T,
        "wdt": a["L0_attn_b_W_dt"].reshape(2, P).T,
        "conv": a["L0_attn_b_conv_w"].reshape(2, P, K).transpose(1, 0, 2),
        "win": a["L0_attn_b_W_in"].T,
        "wout": a["L0_attn_b_W_out"].T.reshape(2, P, D).transpose(1, 0, 2),
        **shape_constants(),
    }
    nc = bacc.Bacc("TRN2", target_bir_lowering=False, num_devices=1)
    args, given = [], {}
    for name, v in arrays.items():
        v = np.ascontiguousarray(v)
        given[f"in_{name}"] = v
        args.append(nc.dram_tensor(f"in_{name}", v.shape, mybir.dt.from_np(v.dtype), kind="ExternalInput").ap())
    out = nc.dram_tensor("out_x", (B, L, D), F32, kind="ExternalOutput").ap()
    hybrid_block_kernel(nc, *args, out)
    r = run_bass_kernel_spmd(nc, [given], core_ids=[0])
    return r.results[0]["out_x"]
```

```python
from contextlib import ExitStack

import numpy as np
import concourse.bass as bass
from concourse import mybir

ALU = mybir.AluOpType
ACT = mybir.ActivationFunctionType
AX = mybir.AxisListType
F32 = mybir.dt.float32
F16 = mybir.dt.float16
I32 = mybir.dt.int32
BF16 = mybir.dt.bfloat16

P = 128
D = 128
B = 4
L = 512
TT = L // P
H = 16
HD = D // H
G = 4
Q = 4
W = 32
PAIRS = 2
W2 = 64
MAX_AT = 6 * HD
E = 8
X = E + 1
F = 512
C = F // P
N = 16
ED = 256
K = 3
EPS = 1e-5
NEG_ROOT = 100.0
LNS = 4
FFNS = 2
S_UNITS = G * TT * Q
T_UNITS = G * TT * 2
PRODUCTS = [(0, 0), (1, 0), (0, 1)]
ORDER = [E] + list(range(E))
GATE_PAD = 16
ATTN_LINKS = 19
FFN_LINKS = 22
SCAN_LINKS = 9
X_SCALE = 2.0 ** 12
TOP = 2.0 ** 14
EXPONENT = 0x7F800000
TINY = 2.0 ** -60


def hybrid_block_kernel(nc, x_in, wqkv_in, wo_in, bo_in, w1_in, b1_in, w2_in, b2_in, wg_in, bg_in, bias_in,
                        a_in, bm_in, cm_in, dv_in, wdt_in, conv_in, win_in, wout_in,
                        cos_in, sin_in, ident_in, neg_eye_in, mask_qk_in, mask_kq_in, pick_in, out):
    with ExitStack() as ctx:
        def sb(name, shape, dt=F32):
            return ctx.enter_context(nc.sbuf_tensor(name, shape, dt))

        def sem(name):
            return ctx.enter_context(nc.semaphore(name))

        ps = ctx.enter_context(nc.psum_tensor("ps", [P, 8, 512], F32))

        wqkv = sb("wqkv", [P, 3 * D])
        wo = sb("wo", [P, D])
        bo = sb("bo", [1, D])
        w1 = sb("w1", [P, 2, X, F], F16)
        b1 = sb("b1", [P, X * C])
        w2 = sb("w2", [P, 2, X, C, D], F16)
        b2 = sb("b2", [P, X])
        wg = sb("wg", [P, E])
        gate_rows = sb("gate_rows", [1, 2, E])
        a_mat = sb("a_mat", [P, 2, N])
        bm = sb("bm", [P, 2, N])
        cm = sb("cm", [N, ED])
        dv = sb("dv", [P, 2])
        wdt = sb("wdt", [P, 2])
        conv = sb("conv", [P, 2, K])
        win = sb("win", [P, 2 * ED])
        wout = sb("wout", [P, 2, D])
        cos = sb("cos", [P, TT, 2, HD])
        sin = sb("sin", [P, TT, 2, HD])
        ident = sb("ident", [P, P])
        ident16 = sb("ident16", [P, P], BF16)
        neg_eye = sb("neg_eye", [P, P], BF16)
        mask_qk = sb("mask_qk", [P, P], BF16)
        mask_kq = sb("mask_kq", [P, P], BF16)
        pick = sb("pick", [3 * E, E, P], BF16)
        ones = sb("ones", [1, P])
        mean_w = sb("mean_w", [P, N])
        minus_half = sb("minus_half", [P, TT])
        wb_mat = sb("wb_mat", [P, 2, N])
        wa = sb("wa", [N, 1])

        xin = sb("xin", [P, TT, D])
        x = sb("x", [P, TT, D])
        xout = sb("xout", [P, TT, D])
        stats = sb("stats", [P, TT, 6])
        mean_sum = sb("mean_sum", [P, TT])
        mean_dif = sb("mean_dif", [P, TT])
        sq_sum = sb("sq_sum", [P, TT])
        mean = sb("mean", [P, TT])
        spacer = sb("spacer", [P, 1])
        var_eps = sb("var_eps", [P, TT])
        rstd = sb("rstd", [P, TT])
        xn = sb("xn", [P, TT, D])
        xnT = sb("xnT", [P, L])

        rope_c = sb("rope_c", [P, TT, 2 * D])
        rope_s = sb("rope_s", [P, TT, 2 * D])
        qk_tok = sb("qk_tok", [P, 2, TT, H, W2], BF16)
        row_maxima = sb("row_maxima", [P, TT, H])
        max_rest = sb("max_rest", [P, TT, Q])
        v_tok = sb("v_tok", [P, TT, H, W])
        kT = sb("kT", [P, G, PAIRS, L], BF16)
        q1T = sb("q1T", [P, G, PAIRS, L], BF16)
        q2T = sb("q2T", [P, G, PAIRS, L], BF16)
        probs = sb("probs", [P, 3, 2, L])
        oT = sb("oT", [P, G, L])
        rec = sb("rec", [P, TT, H])
        att = sb("att", [P, TT, D])
        attT = sb("attT", [P, L])

        score = sb("score", [P, TT, GATE_PAD])
        best = sb("best", [P, TT, 8])
        taken = sb("taken", [P, TT, 8])
        left = sb("left", [P, TT, GATE_PAD])
        route = sb("route", [P, TT, E])
        rest = sb("rest", [P, TT, E])
        part = sb("part", [P, TT, 3 * E], BF16)
        partT = sb("partT", [3 * E, L], BF16)
        x16 = sb("x16", [P, 2, L], F16)
        arena = sb("arena", [P, 12288])
        w1_raw = arena[:, 0:X * F].rearrange("p (e f) -> p e f", e=X)
        w2_raw = arena[:, X * F:2 * X * F].rearrange("p (e c d) -> p e c d", e=X, c=C)
        wide = arena[:, 0:E * L].rearrange("p (e l) -> p e l", e=E)
        hid = arena[:, 4096:8192].rearrange("p (s c l) -> p s c l", s=2, c=C)
        hid16 = arena[:, 8192:12288].bitcast(F16).rearrange("p (s k c l) -> p s k c l", s=2, k=2, c=C)
        tops = sb("tops", [P, 4])
        bounds = sb("bounds", [P, 4])
        powers = sb("powers", [P, 4])
        inverses = sb("inverses", [P, 4])
        up_scale = sb("up_scale", [P, 1])
        down_scale = sb("down_scale", [P, 1])
        hid_scale = sb("hid_scale", [P, 1])
        up_back = sb("up_back", [P, 1])
        down_back = sb("down_back", [P, 1])
        back_root = sb("back_root", [P, 1])
        b2_scaled = sb("b2_scaled", [P, X])
        tmp = sb("tmp", [P, 2, L])
        acc = sb("acc", [P, L])

        xs, xcv = (arena[:, 4096 + 1024 * i:4096 + 1024 * (i + 1)].rearrange("p (c l) -> p c l", c=2) for i in range(2))
        decay, u_raw, u_in, state = (arena[0:N, 6144 + L * i:6144 + L * (i + 1)] for i in range(4))
        y, gate, diff, z = (wide[:, 2 * i:2 * i + 2, :] for i in range(4))

        consts_in = sem("consts_in")
        ffn_in = sem("ffn_in")
        scan_in = sem("scan_in")
        pads_set = sem("pads_set")
        prep_step = sem("prep_step")
        attn_step = sem("attn_step")
        ffn_step = sem("ffn_step")
        scan_step = sem("scan_step")
        tops_found = sem("tops_found")
        bounds_ready = sem("bounds_ready")
        scales_ready = sem("scales_ready")
        high_ready = sem("high_ready")
        low_ready = sem("low_ready")
        x16_ready = sem("x16_ready")
        hid16_ready = sem("hid16_ready")
        xin_ready = sem("xin_ready")
        xin_free = sem("xin_free")
        out_ready = sem("out_ready")
        out_stored = sem("out_stored")
        var_ready = sem("var_ready")
        rstd_ready = sem("rstd_ready")
        xn_ready = sem("xn_ready")
        xnT_made = sem("xnT_made")
        xnT_ready = sem("xnT_ready")
        v_made = sem("v_made")
        v_ready = sem("v_ready")
        qk_made = sem("qk_made")
        roped = sem("roped")
        kT_made = sem("kT_made")
        kT_ready = sem("kT_ready")
        q1T_made = sem("q1T_made")
        q1T_ready = sem("q1T_ready")
        score_made = sem("score_made")
        max_ready = sem("max_ready")
        max_split = sem("max_split")
        q2T_made = sem("q2T_made")
        q2T_ready = sem("q2T_ready")
        st_made = sem("st_made")
        exp_ready = sem("exp_ready")
        pv_made = sem("pv_made")
        o_ready = sem("o_ready")
        otok_made = sem("otok_made")
        att_ready = sem("att_ready")
        attT_made = sem("attT_made")
        attT_ready = sem("attT_ready")
        wo_made = sem("wo_made")
        gate_made = sem("gate_made")
        sig_ready = sem("sig_ready")
        part_ready = sem("part_ready")
        partT_made = sem("partT_made")
        partT_ready = sem("partT_ready")
        wide_made = sem("wide_made")
        wide_ready = sem("wide_ready")
        up_made = sem("up_made")
        gelu_ready = sem("gelu_ready")
        down_made = sem("down_made")
        down_read = sem("down_read")
        acc_ready = sem("acc_ready")
        accT_made = sem("accT_made")
        wa_made = sem("wa_made")
        wa_ready = sem("wa_ready")
        wb_ready = sem("wb_ready")
        proj_made = sem("proj_made")
        xs_ready = sem("xs_ready")
        dtu_made = sem("dtu_made")
        u_ready = sem("u_ready")
        state_ready = sem("state_ready")
        y_made = sem("y_made")
        y_ready = sem("y_ready")
        gate_ready = sem("gate_ready")
        z_ready = sem("z_ready")
        mo_made = sem("mo_made")

        x_dram = x_in.rearrange("b (t p) d -> b p t d", p=P)
        out_dram = out.rearrange("b (t p) d -> b p t d", p=P)

        attn_loads = [(wqkv, wqkv_in), (cos, cos_in), (sin, sin_in), (ident, ident_in), (wo, wo_in), (bo, bo_in),
                      (neg_eye, neg_eye_in), (mask_qk, mask_qk_in), (mask_kq, mask_kq_in)]
        ffn_loads = [(wg, wg_in), (gate_rows[:, 0, :], bg_in), (gate_rows[:, 1, :], bias_in), (w1_raw, w1_in),
                     (b1, b1_in), (w2_raw, w2_in), (b2, b2_in), (pick, pick_in)]
        scan_loads = [(a_mat, a_in), (bm, bm_in), (cm, cm_in), (dv, dv_in), (wdt, wdt_in), (conv, conv_in),
                      (win, win_in), (wout, wout_in)]

        block = ctx.enter_context(nc.Block())

        def whole(t):
            return t[:] if not isinstance(t, bass.AP) else t

        @block.sync
        def _(sp):
            for dst, src in attn_loads[:4]:
                sp.dma_start(whole(dst), src).then_inc(consts_in, 16)
            sp.dma_start(xin[:], x_dram[0]).then_inc(xin_ready, 16)
            for dst, src in attn_loads[4:]:
                sp.dma_start(whole(dst), src).then_inc(consts_in, 16)
            for dst, src in ffn_loads:
                sp.dma_start(whole(dst), src).then_inc(ffn_in, 16)
            for dst, src in scan_loads:
                sp.dma_start(whole(dst), src).then_inc(scan_in, 16)
            with sp.Fori(1, B) as b:
                sp.wait_ge(xin_free, b)
                sp.dma_start(xin[:], x_dram[bass.ds(b, 1)].rearrange("o p t d -> (o p) t d")).then_inc(xin_ready, 16)

        @block.gpsimd
        def _(pool):
            nc.gpsimd.memset(minus_half[:], -0.5).then_inc(pads_set, 1)
            nc.gpsimd.memset(v_tok[:], 0.0)
            nc.gpsimd.memset(score[:], -1.0).then_inc(o_ready, 1)
            nc.gpsimd.memset(taken[:], -1.0).then_inc(out_stored, 16)
            nc.gpsimd.memset(ones[:], 1.0)
            nc.gpsimd.memset(mean_w[:], 1.0 / ED).then_inc(pads_set, 1)
            pool.wait_ge(pads_set, 2)
            nc.gpsimd.memset(v_tok[:, :, :, HD:HD + 1], 1.0).then_inc(pads_set, 1)
            pool.wait_ge(tops_found, 1)
            nc.gpsimd.partition_all_reduce(bounds[:, 0:3], tops[:, 0:3], P,
                                           bass.bass_isa.ReduceOp.max).then_inc(bounds_ready, 1)
            with pool.Fori(0, B) as b:
                for r in range(LNS):
                    pool.wait_ge(var_ready, b * LNS + r + 1)
                    nc.gpsimd.tensor_tensor(rstd[:], var_eps[:], minus_half[:], ALU.pow).then_inc(rstd_ready, 1)

        @block.scalar
        def _(act):
            def norm_T(b, r):
                act.wait_ge(xnT_made, b * LNS + r + 1)
                nc.scalar.copy(xnT[:], ps[:, 0, :]).then_inc(xnT_ready, 1)

            def attention(b):
                norm_T(b, 0)
                act.wait_ge(v_made, b + 1)
                act.wait_ge(pads_set, 3)
                nc.scalar.copy(v_tok[:, :, :, 0:HD],
                               ps[:, 1, :].rearrange("p (t h d) -> p t h d", t=TT, h=H)).then_inc(v_ready, 1)
                for g in range(G):
                    act.wait_ge(kT_made, b * G + g + 1)
                    nc.scalar.copy(kT[:, g].rearrange("p a l -> p (a l)"), ps[:, g, :].bitcast(BF16)).then_inc(kT_ready, 1)
                for g in range(G):
                    act.wait_ge(q2T_made, b * G + g + 1)
                    nc.scalar.copy(q2T[:, g].rearrange("p a l -> p (a l)"), ps[:, 7, :].bitcast(BF16)).then_inc(q2T_ready, 1)
                    for j in range(TT):
                        for pr in range(2):
                            m = (g * TT + j) * 2 + pr
                            n = L - P * j
                            bank = 2 + 2 * (m % 2)
                            act.wait_ge(st_made, b * T_UNITS + m + 1)
                            if m >= 3:
                                act.wait_ge(pv_made, b * T_UNITS + m - 2)
                            nc.scalar.activation(probs[:, m % 3, :, 0:n], ps[:, bank:bank + 2, 0:n],
                                                 ACT.Exp).then_inc(exp_ready, 1)
                act.wait_ge(attT_made, b + 1)
                nc.scalar.copy(attT[:], ps[:, 4, :]).then_inc(attT_ready, 1)

            def ffn(b, r):
                f = b * FFNS + r
                norm_T(b, 1 + 2 * r)
                act.wait_ge(gate_made, f + 1)
                act.wait_ge(pads_set, 3)
                nc.scalar.activation(score[:, :, 0:E], ps[:, 1, 0:TT * E].rearrange("p (t e) -> p t e", t=TT),
                                     ACT.Sigmoid).then_inc(sig_ready, 1)

                def wide_copy(e):
                    act.wait_ge(wide_made, f * E + e + 1)
                    nc.scalar.activation(wide[:, e, :], ps[:, 2 + e % 2, :], ACT.Identity,
                                         scale=down_back[:]).then_inc(wide_ready, 1)

                for i in range(X):
                    for c in range(C):
                        n = i * C + c
                        act.wait_ge(up_made, f * X * C + n + 1)
                        if i >= 2 and c == 0:
                            act.wait_ge(hid16_ready, f * X + i - 1)
                        nc.scalar.activation(hid[:, i % 2, c, :], ps[:, 4 + n % 2, :], ACT.Gelu,
                                             bias=b1[:, ORDER[i] * C + c:ORDER[i] * C + c + 1],
                                             scale=up_back[:]).then_inc(gelu_ready, 1)
                    if i == 1:
                        act.wait_ge(partT_made, f + 1)
                        nc.scalar.copy(partT[:], ps[0:3 * E, 0, 0:L // 2].bitcast(BF16)).then_inc(partT_ready, 1)
                    if i == 2:
                        wide_copy(0)
                        wide_copy(1)
                    if i >= 3:
                        wide_copy(i - 1)

            def scan_block(b):
                norm_T(b, 2)
                for c in range(2):
                    act.wait_ge(proj_made, b * 4 + c + 1)
                    nc.scalar.copy(xs[:, c, :], ps[:, 3 + c, :]).then_inc(xs_ready, 1)
                act.wait_ge(dtu_made, b + 1)
                nc.scalar.copy(u_raw, ps[0:N, 6, :]).then_inc(u_ready, 1)
                act.wait_ge(y_ready, b + 1)
                nc.scalar.activation(gate, y, ACT.Sigmoid).then_inc(gate_ready, 1)

            act.wait_ge(ffn_in, 16 * len(ffn_loads))
            act.wait_ge(scales_ready, 1)
            nc.scalar.activation(w1[:, 0], w1_raw, ACT.Identity, scale=up_scale[:]).then_inc(high_ready, 1)
            nc.scalar.activation(w2[:, 0], w2_raw, ACT.Identity, scale=down_scale[:]).then_inc(high_ready, 1)
            act.wait_ge(wa_made, 1)
            nc.scalar.copy(wa[:], ps[0:N, 7, 0:1]).then_inc(wa_ready, 1)
            with act.Fori(0, B) as b:
                attention(b)
                ffn(b, 0)
                scan_block(b)
                ffn(b, 1)
                act.wait_ge(out_ready, b + 1)
                act.dma_start(out_dram[bass.ds(b, 1)].rearrange("o p t d -> (o p) t d"),
                              xout[:]).then_inc(out_stored, 16)
            act.wait_ge(out_stored, 16 * B + 16)

        @block.tensor
        def _(pe):
            def norm_T(b, r):
                pe.wait_ge(xn_ready, b * LNS + r + 1)
                for t in range(TT):
                    mm = pe.transpose(ps[:, 0, t * P:(t + 1) * P], xn[:, t, :], ident[:])
                mm.then_inc(xnT_made, 1)
                pe.wait_ge(xnT_ready, b * LNS + r + 1)

            def scores(b, g, t, q):
                n = (g * TT + t) * Q + q
                keys = P * (t + 1)
                if n >= 2:
                    pe.wait_ge(max_ready, b * S_UNITS + n - 1)
                r = W2 * (q % 2)
                pe.matmul(ps[:, n % 2, 0:keys], q1T[r:r + MAX_AT, g, q // 2, t * P:(t + 1) * P],
                          kT[r:r + MAX_AT, g, q // 2, 0:keys], start=True, stop=False)
                pe.matmul(ps[:, n % 2, keys - P:keys], neg_eye[:], mask_qk[:],
                          start=False, stop=True).then_inc(score_made, 1)

            def heads_T(bank, k, g):
                to = ps[:, bank, :].bitcast(BF16).rearrange("p (a l) -> p a l", a=PAIRS)
                for a in range(PAIRS):
                    for t in range(TT):
                        h = Q * g + 2 * a
                        mm = pe.transpose(to[:, a, t * P:(t + 1) * P],
                                          qk_tok[:, k, t, h:h + 2, :].rearrange("p h w -> p (h w)"), ident16[:])
                return mm

            def queries_with_max(b, g):
                pe.wait_ge(max_split, b * G + g + 1)
                heads_T(7, 0, g).then_inc(q2T_made, 1)

            def scores_T(b, m):
                g, j, pr = m // (2 * TT), m // 2 % TT, m % 2
                n = L - P * j
                bank = 2 + 2 * (m % 2)
                if m % (2 * TT) == 0:
                    pe.wait_ge(q2T_ready, b * G + g + 1)
                if m >= 2:
                    pe.wait_ge(exp_ready, b * T_UNITS + m - 1)
                for h in range(2):
                    r = W2 * h
                    pe.matmul(ps[:, bank + h, 0:n], kT[r:r + W2, g, pr, j * P:(j + 1) * P],
                              q2T[r:r + W2, g, pr, j * P:L], start=True, stop=False)
                for h in range(2):
                    mm = pe.matmul(ps[:, bank + h, 0:P], neg_eye[:], mask_kq[:], start=False, stop=True)
                mm.then_inc(st_made, 1)

            def weigh_values(b, m):
                g, j, pr = m // (2 * TT), m // 2 % TT, m % 2
                n = L - P * j
                if m % (2 * TT) == 0:
                    pe.wait_ge(o_ready, b * G + g + 1)
                pe.wait_ge(exp_ready, b * T_UNITS + m + 1)
                for h in range(2):
                    r = 2 * pr + h
                    mm = pe.matmul(ps[W * r:W * r + W, 6, j * P:L], v_tok[:, j, Q * g + r, :],
                                   probs[:, m % 3, h, 0:n], start=(j == 0), stop=(j == TT - 1))
                mm.then_inc(pv_made, 1)

            def attention(b):
                norm_T(b, 0)
                for t in range(TT):
                    pe.matmul(ps[:, 4 + t, 0:2 * D], xnT[:, t * P:(t + 1) * P], wqkv[:, 0:2 * D],
                              start=True, stop=True).then_inc(qk_made, 1)
                for t in range(TT):
                    mm = pe.matmul(ps[:, 1, t * D:(t + 1) * D], xnT[:, t * P:(t + 1) * P], wqkv[:, 2 * D:3 * D],
                                   start=True, stop=True)
                mm.then_inc(v_made, 1)
                pe.wait_ge(roped, b + 1)
                pe.wait_ge(v_ready, b + 1)
                for g in range(G):
                    heads_T(g, 1, g).then_inc(kT_made, 1)
                    heads_T(4 + g, 0, g).then_inc(q1T_made, 1)
                pe.wait_ge(kT_ready, b * G + G)
                pe.wait_ge(q1T_ready, b * G + G)
                for u in range(TT * Q):
                    scores(b, 0, u // Q, u % Q)
                per = 2 * TT
                for g in range(G):
                    queries_with_max(b, g)
                    scores_T(b, g * per)
                    for i in range(per):
                        if g + 1 < G:
                            for u in (2 * i, 2 * i + 1):
                                scores(b, g + 1, u // Q, u % Q)
                        if i + 1 < per:
                            scores_T(b, g * per + i + 1)
                        weigh_values(b, g * per + i)
                pe.wait_ge(o_ready, b * G + G + 1)
                for t in range(TT):
                    for g in range(G):
                        mm = pe.transpose(ps[:, t, g * P:(g + 1) * P], oT[:, g, t * P:(t + 1) * P], ident[:])
                    mm.then_inc(otok_made, 1)
                pe.wait_ge(att_ready, b + 1)
                for t in range(TT):
                    mm = pe.transpose(ps[:, 4, t * P:(t + 1) * P], att[:, t, :], ident[:])
                mm.then_inc(attT_made, 1)
                pe.wait_ge(attT_ready, b + 1)
                for t in range(TT):
                    pe.matmul(ps[:, 5, t * D:(t + 1) * D], attT[:, t * P:(t + 1) * P], wo[:], start=True, stop=False)
                    mm = pe.matmul(ps[:, 5, t * D:(t + 1) * D], ones[:], bo[:], start=False, stop=True)
                mm.then_inc(wo_made, 1)

            def ffn(b, r):
                f = b * FFNS + r
                norm_T(b, 1 + 2 * r)
                for t in range(TT):
                    o = ps[:, 1, t * E:(t + 1) * E]
                    pe.matmul(o, xnT[:, t * P:(t + 1) * P], wg[:], start=True, stop=False)
                    pe.matmul(o, ones[:], gate_rows[:, 0, :], start=False, stop=False)
                    mm = pe.matmul(o, ones[:], gate_rows[:, 1, :], start=False, stop=True)
                mm.then_inc(gate_made, 1)

                def up(i, c):
                    n = i * C + c
                    if n >= 2:
                        pe.wait_ge(gelu_ready, f * X * C + n - 1)
                    for k, (w, v) in enumerate(PRODUCTS):
                        mm = pe.matmul(ps[:, 4 + n % 2, :], w1[:, w, ORDER[i], c * P:(c + 1) * P], x16[:, v, :],
                                       start=(k == 0), stop=(k == 2))
                    mm.then_inc(up_made, 1)

                def down(i, c):
                    if c == 0:
                        if i >= 2:
                            pe.wait_ge(down_read, f * X + i - 1)
                        pe.wait_ge(hid16_ready, f * X + i + 1)
                    for k, (w, v) in enumerate(PRODUCTS):
                        mm = pe.matmul(ps[:, 6 + i % 2, :], w2[:, w, ORDER[i], c, :], hid16[:, i % 2, v, c, :],
                                       start=(c == 0 and k == 0), stop=(c == C - 1 and k == 2))
                    if c == C - 1:
                        mm.then_inc(down_made, 1)

                def widen(e):
                    if e >= 2:
                        pe.wait_ge(wide_ready, f * E + e - 1)
                    pe.matmul(ps[:, 2 + e % 2, :], pick[:, e, :], partT[:], start=True,
                              stop=True).then_inc(wide_made, 1)

                pe.wait_ge(x16_ready, f + 1)
                for c in range(C):
                    up(0, c)
                for i in range(X):
                    if i + 1 < X:
                        for c in range(C):
                            up(i + 1, c)
                    for c in range(C):
                        down(i, c)
                    if i == 0:
                        pe.wait_ge(part_ready, f + 1)
                        for t in range(TT):
                            mm = pe.transpose(ps[0:3 * E, 0, t * (P // 2):(t + 1) * (P // 2)].bitcast(BF16),
                                              part[:, t, :], ident16[:])
                        mm.then_inc(partT_made, 1)
                    if i == 1:
                        pe.wait_ge(partT_ready, f + 1)
                        widen(0)
                        widen(1)
                    if 2 <= i < E:
                        widen(i)
                pe.wait_ge(acc_ready, f * E + E)
                for t in range(TT):
                    mm = pe.transpose(ps[:, 1, t * P:(t + 1) * P], acc[:, t * P:(t + 1) * P], ident[:])
                mm.then_inc(accT_made, 1)

            def scan_block(b):
                norm_T(b, 2)
                for n, k in enumerate((2, 3, 0, 1)):
                    pe.matmul(ps[:, 1 + k, :], win[:, k * P:(k + 1) * P], xnT[:], start=True,
                              stop=True).then_inc(proj_made, 1)
                pe.wait_ge(xs_ready, b * 2 + 2)
                for c in range(2):
                    pe.matmul(ps[0:N, 6, :], wb_mat[:, c, :], xs[:, c, :], start=(c == 0), stop=(c == 1))
                for c in range(2):
                    mm = pe.matmul(ps[0:N, 5, :], mean_w[:], xs[:, c, :], start=(c == 0), stop=(c == 1))
                mm.then_inc(dtu_made, 1)
                pe.wait_ge(state_ready, b + 1)
                for c in range(2):
                    pe.matmul(ps[:, 7 * (1 - c), :], cm[:, c * P:(c + 1) * P], state, start=True,
                              stop=True).then_inc(y_made, 1)
                pe.wait_ge(z_ready, b + 1)
                for t in range(TT):
                    for c in range(2):
                        mm = pe.matmul(ps[:, 1, t * D:(t + 1) * D], z[:, c, t * P:(t + 1) * P], wout[:, c, :],
                                       start=(c == 0), stop=(c == 1))
                mm.then_inc(mo_made, 1)

            pe.wait_ge(scan_in, 16 * len(scan_loads))
            for c in range(2):
                mm = pe.matmul(ps[0:N, 7, 0:1], a_mat[:, c, :], wdt[:, c:c + 1], start=(c == 0), stop=(c == 1))
            mm.then_inc(wa_made, 1)
            pe.wait_ge(wa_ready, 1)
            pe.wait_ge(consts_in, 16 * len(attn_loads))
            pe.wait_ge(ffn_in, 16 * len(ffn_loads))
            pe.wait_ge(pads_set, 3)
            pe.wait_ge(wb_ready, 1)
            pe.wait_ge(low_ready, 2)
            with pe.Fori(0, B) as b:
                attention(b)
                ffn(b, 0)
                scan_block(b)
                ffn(b, 1)

        @block.vector
        def _(dve):
            class Links:
                def __init__(self, semaphore, per_stage):
                    self.semaphore, self.per_stage, self.n = semaphore, per_stage, 0

                def __call__(self, stage, ins):
                    self.n += 1
                    ins.then_inc(self.semaphore, 1)
                    dve.wait_ge(self.semaphore, stage * self.per_stage + self.n)

                def end(self):
                    assert self.n == self.per_stage, self.n
                    self.n = 0

            attn_link = Links(attn_step, ATTN_LINKS)
            ffn_link = Links(ffn_step, FFN_LINKS)
            scan_link = Links(scan_step, SCAN_LINKS)

            def norm(b, r, src, link, stage):
                for t in range(TT):
                    ins = nc.vector.bn_stats(stats[:, t, :], src[:, t, :])
                link(stage, ins)
                mean_e, sq_e, mean_o, sq_o = (stats[:, :, i] for i in (1, 2, 4, 5))
                nc.vector.tensor_tensor(mean_sum[:], mean_e, mean_o, ALU.add)
                nc.vector.tensor_tensor(mean_dif[:], mean_e, mean_o, ALU.subtract)
                link(stage, nc.vector.scalar_tensor_tensor(sq_sum[:], sq_e, D * EPS, sq_o, ALU.add, ALU.add))
                nc.vector.tensor_scalar(mean[:], mean_sum[:], 0.5, None, ALU.mult)
                link(stage, nc.vector.scalar_tensor_tensor(mean_dif[:], mean_dif[:], 0.25, mean_dif[:], ALU.mult, ALU.mult))
                nc.vector.scalar_tensor_tensor(var_eps[:], sq_sum[:], 1.0 / D, mean_dif[:], ALU.mult,
                                               ALU.add).then_inc(var_ready, 1)
                dve.wait_ge(rstd_ready, b * LNS + r + 1)
                for t in range(TT):
                    ins = nc.vector.tensor_scalar(xn[:, t, :], src[:, t, :], mean[:, t:t + 1], rstd[:, t:t + 1],
                                                  ALU.subtract, ALU.mult)
                ins.then_inc(xn_ready, 1)

            def row_max(b, g):
                for t in range(TT):
                    for q in range(Q):
                        n = (g * TT + t) * Q + q
                        dve.wait_ge(score_made, b * S_UNITS + n + 1)
                        nc.vector.tensor_reduce(row_maxima[:, t, Q * g + q:Q * g + q + 1],
                                                ps[:, n % 2, 0:P * (t + 1)], AX.X, ALU.max).then_inc(max_ready, 1)
                heads = slice(Q * g, Q * g + Q)
                dve.wait_ge(max_ready, b * S_UNITS + TT * Q * (g + 1))
                attn_link(b, nc.vector.tensor_copy(qk_tok[:, 0, :, heads, MAX_AT], row_maxima[:, :, heads]))
                attn_link(b, nc.vector.tensor_tensor(max_rest[:], row_maxima[:, :, heads],
                                                     qk_tok[:, 0, :, heads, MAX_AT], ALU.subtract))
                nc.vector.tensor_copy(qk_tok[:, 0, :, heads, MAX_AT + 1], max_rest[:]).then_inc(max_split, 1)

            def attention(b):
                dve.wait_ge(xin_ready, b * 16 + 16)
                norm(b, 0, xin, attn_link, b)
                for t in range(TT):
                    dve.wait_ge(qk_made, b * TT + t + 1)
                    qk = ps[:, 4 + t, 0:2 * D]

                    def by_head(a):
                        return a.rearrange("p (k h d) -> p k h d", k=2, h=H)

                    def all_heads(table, part):
                        a = table[:, t, :, part]
                        return a.unsqueeze(2).broadcast_to([P, 2, H, a.shape[2]])

                    even, odd = slice(0, HD, 2), slice(1, HD, 2)
                    nc.vector.tensor_tensor(by_head(rope_c[:, t, :]), by_head(qk), all_heads(cos, slice(0, HD)), ALU.mult)
                    for to, of in ((even, odd), (odd, even)):
                        ins = nc.vector.tensor_tensor(by_head(rope_s[:, t, :])[:, :, :, to], by_head(qk)[:, :, :, of],
                                                      all_heads(sin, to), ALU.mult)
                attn_link(b, ins)
                attn_link(b, nc.vector.tensor_tensor(rope_c[:], rope_c[:], rope_s[:], ALU.add))
                qk32 = rope_c[:].rearrange("p t (k h d) -> p k t h d", k=2, h=H)
                rest = rope_s[:].rearrange("p t (k h d) -> p k t h d", k=2, h=H)

                def slot(k, n):
                    return qk_tok[:, k, :, :, n * HD:(n + 1) * HD]

                for k in range(2):
                    ins = nc.vector.tensor_copy(slot(k, 0), qk32[:, k])
                attn_link(b, ins)
                for k in range(2):
                    ins = nc.vector.tensor_tensor(rest[:, k], qk32[:, k], slot(k, 0), ALU.subtract)
                attn_link(b, ins)
                for k in range(2):
                    ins = nc.vector.tensor_copy(slot(k, 1), rest[:, k])
                attn_link(b, ins)
                for k in range(2):
                    ins = nc.vector.tensor_tensor(rest[:, k], rest[:, k], slot(k, 1), ALU.subtract)
                attn_link(b, ins)
                nc.vector.tensor_copy(slot(0, 5), rest[:, 0])
                nc.vector.tensor_copy(slot(1, 4), rest[:, 1])
                nc.vector.tensor_copy(slot(0, 2), slot(0, 0))
                nc.vector.tensor_copy(slot(0, 4), slot(0, 0))
                nc.vector.tensor_copy(slot(1, 3), slot(1, 0))
                nc.vector.tensor_copy(slot(1, 5), slot(1, 0))
                nc.vector.tensor_copy(slot(0, 3), slot(0, 1))
                nc.vector.tensor_copy(slot(1, 2), slot(1, 1)).then_inc(roped, 1)
                for g in range(G):
                    dve.wait_ge(q1T_made, b * G + g + 1)
                    nc.vector.tensor_copy(q1T[:, g].rearrange("p a l -> p (a l)"),
                                          ps[:, 4 + g, :].bitcast(BF16)).then_inc(q1T_ready, 1)
                row_max(b, 0)
                for g in range(G):
                    if g + 1 < G:
                        row_max(b, g + 1)
                    dve.wait_ge(pv_made, b * T_UNITS + 2 * TT * (g + 1))
                    nc.vector.tensor_copy(oT[:, g, :], ps[:, 6, :]).then_inc(o_ready, 1)
                for t in range(TT):
                    dve.wait_ge(otok_made, b * TT + t + 1)
                    ins = nc.vector.reciprocal(rec[:, t, :], ps[:, t, :].rearrange("p (h w) -> p h w", w=W)[:, :, HD])
                attn_link(b, ins)
                for t in range(TT):
                    ins = nc.vector.tensor_tensor(
                        att[:, t, :].rearrange("p (h d) -> p h d", h=H),
                        ps[:, t, :].rearrange("p (h w) -> p h w", w=W)[:, :, 0:HD],
                        rec[:, t, :].unsqueeze(2).broadcast_to([P, H, HD]), ALU.mult)
                ins.then_inc(att_ready, 1)
                dve.wait_ge(wo_made, b + 1)
                ins = nc.vector.tensor_tensor(x[:].rearrange("p t d -> p (t d)"), ps[:, 5, :],
                                              xin[:].rearrange("p t d -> p (t d)"), ALU.add)
                attn_link(b, ins)
                nc.vector.tensor_copy(rec[:, 0, 0:1], x[:, 0, 0:1]).then_inc(xin_free, 1)
                attn_link.end()

            def ffn(b, r):
                f = b * FFNS + r
                norm(b, 1 + 2 * r, x, ffn_link, f)
                dve.wait_ge(xnT_ready, b * LNS + 2 * r + 2)
                ffn_link(f, nc.vector.tensor_scalar(x16[:, 0, :], xnT[:], X_SCALE, None, ALU.mult))
                nc.vector.scalar_tensor_tensor(x16[:, 1, :], xnT[:], X_SCALE, x16[:, 0, :], ALU.mult,
                                               ALU.subtract).then_inc(x16_ready, 1)
                dve.wait_ge(sig_ready, f + 1)
                nc.vector.memset(spacer[:], 0.0)
                for t in range(TT):
                    ins = nc.vector.max(best[:, t, :], score[:, t, :])
                ffn_link(f, ins)
                ffn_link(f, nc.vector.tensor_copy(taken[:, :, 0:2], best[:, :, 0:2]))
                nc.vector.memset(spacer[:], 0.0)
                for t in range(TT):
                    ins = nc.vector.match_replace(left[:, t, :], taken[:, t, :], score[:, t, :], 0.0)
                ffn_link(f, ins)
                ffn_link(f, nc.vector.tensor_tensor(route[:], score[:, :, 0:E], left[:, :, 0:E], ALU.subtract))
                ffn_link(f, nc.vector.tensor_copy(part[:, :, 0:E], route[:]))
                ffn_link(f, nc.vector.tensor_tensor(rest[:], route[:], part[:, :, 0:E], ALU.subtract))
                ffn_link(f, nc.vector.tensor_copy(part[:, :, E:2 * E], rest[:]))
                ffn_link(f, nc.vector.tensor_tensor(route[:], rest[:], part[:, :, E:2 * E], ALU.subtract))
                nc.vector.tensor_copy(part[:, :, 2 * E:3 * E], route[:]).then_inc(part_ready, 1)

                def split_hidden(i):
                    dve.wait_ge(gelu_ready, f * X * C + (i + 1) * C)
                    if i >= 2:
                        dve.wait_ge(down_made, f * X + i - 1)
                    src, high, low = hid[:, i % 2], hid16[:, i % 2, 0], hid16[:, i % 2, 1]
                    ffn_link(f, nc.vector.tensor_scalar(high, src, hid_scale[:], None, ALU.mult))
                    nc.vector.scalar_tensor_tensor(low, src, hid_scale[:], high, ALU.mult,
                                                   ALU.subtract).then_inc(hid16_ready, 1)

                def combine(i):
                    e = ORDER[i]
                    dve.wait_ge(down_made, f * X + i + 1)
                    if i == 0:
                        nc.vector.tensor_scalar(acc[:], ps[:, 6, :], down_back[:], b2[:, e:e + 1],
                                                ALU.mult, ALU.add).then_inc(down_read, 1)
                        dve.wait_ge(down_read, f * X + 1)
                        return
                    dve.wait_ge(wide_ready, f * E + e + 1)
                    nc.vector.scalar_tensor_tensor(tmp[:, i % 2, :], ps[:, 6 + i % 2, :], b2_scaled[:, e:e + 1],
                                                   wide[:, e, :], ALU.add, ALU.mult).then_inc(down_read, 1)
                    dve.wait_ge(down_read, f * X + i + 1)
                    nc.vector.tensor_tensor(acc[:], acc[:], tmp[:, i % 2, :], ALU.add).then_inc(acc_ready, 1)
                    dve.wait_ge(acc_ready, f * E + i)

                split_hidden(0)
                for i in range(X):
                    if i + 1 < X:
                        split_hidden(i + 1)
                    combine(i)
                dve.wait_ge(accT_made, f + 1)
                x_flat = x[:].rearrange("p t d -> p (t d)")
                if r == 0:
                    ffn_link(f, nc.vector.tensor_tensor(x_flat, ps[:, 1, :], x_flat, ALU.add))
                else:
                    dve.wait_ge(out_stored, b * 16 + 16)
                    nc.vector.tensor_tensor(xout[:].rearrange("p t d -> p (t d)"), ps[:, 1, :], x_flat,
                                            ALU.add).then_inc(out_ready, 1)
                    ffn_link(f, nc.vector.memset(spacer[:], 0.0))
                ffn_link.end()

            def scan_block(b):
                norm(b, 2, x, scan_link, b)
                x_flat = x[:].rearrange("p t d -> p (t d)")
                dve.wait_ge(xn_ready, b * LNS + 3)
                nc.vector.tensor_tensor(x_flat, x_flat, xn[:].rearrange("p t d -> p (t d)"), ALU.add)
                dve.wait_ge(proj_made, b * 4 + 4)
                for c in range(2):
                    ins = nc.vector.tensor_scalar(xcv[:, c, :], ps[:, 1 + c, :], conv[:, c, 1:2], None, ALU.mult)
                scan_link(b, ins)
                for c in range(2):
                    ins = nc.vector.scalar_tensor_tensor(xcv[:, c, 1:L], ps[:, 1 + c, 0:L - 1], conv[:, c, 0:1],
                                                         xcv[:, c, 1:L], ALU.mult, ALU.add)
                scan_link(b, ins)
                for c in range(2):
                    ins = nc.vector.scalar_tensor_tensor(xcv[:, c, 0:L - 1], ps[:, 1 + c, 1:L], conv[:, c, 2:3],
                                                         xcv[:, c, 0:L - 1], ALU.mult, ALU.add)
                dve.wait_ge(dtu_made, b + 1)
                nc.vector.tensor_scalar(decay, ps[0:N, 5, :], wa[:, 0:1], None, ALU.mult)
                dve.wait_ge(u_ready, b + 1)
                scan_link(b, nc.vector.tensor_tensor(u_in, u_raw, ps[0:N, 5, :], ALU.mult))
                nc.vector.tensor_tensor_scan(state, decay, u_in, 0.0, ALU.mult,
                                             ALU.add).then_inc(state_ready, 1)
                for c in range(2):
                    dve.wait_ge(y_made, b * 2 + c + 1)
                    ins = nc.vector.scalar_tensor_tensor(y[:, c, :], xs[:, c, :], dv[:, c:c + 1],
                                                         ps[:, 7 * (1 - c), :], ALU.mult, ALU.add)
                ins.then_inc(y_ready, 1)
                dve.wait_ge(y_ready, b + 1)
                scan_link(b, nc.vector.tensor_tensor(diff, xcv[:], y, ALU.subtract))
                dve.wait_ge(gate_ready, b + 1)
                scan_link(b, nc.vector.tensor_tensor(diff, diff, gate, ALU.mult))
                nc.vector.tensor_tensor(z, diff, y, ALU.add).then_inc(z_ready, 1)
                dve.wait_ge(mo_made, b + 1)
                scan_link(b, nc.vector.tensor_tensor(x_flat, ps[:, 1, :], x_flat, ALU.add))
                scan_link.end()

            steps = [0]

            def prep(ins):
                steps[0] += 1
                ins.then_inc(prep_step, 1)
                dve.wait_ge(prep_step, steps[0])

            prep(nc.vector.memset(qk_tok[:], 0.0))
            prep(nc.vector.memset(qk_tok[:, 1, :, :, MAX_AT:MAX_AT + 2], -1.0))
            dve.wait_ge(consts_in, 16 * len(attn_loads))
            prep(nc.vector.tensor_copy(ident16[:], ident[:]))
            dve.wait_ge(scan_in, 16 * len(scan_loads))
            for c in range(2):
                ins = nc.vector.tensor_scalar(wb_mat[:, c, :], bm[:, c, :], wdt[:, c:c + 1], None, ALU.mult)
            prep(ins)
            dve.wait_ge(ffn_in, 16 * len(ffn_loads))
            nc.vector.tensor_reduce(tops[:, 0:1], w1_raw.rearrange("p e f -> p (e f)"), AX.X, ALU.max,
                                    apply_absolute_value=True)
            nc.vector.tensor_reduce(tops[:, 1:2], w2_raw.rearrange("p e c d -> p (e c d)"), AX.X, ALU.max,
                                    apply_absolute_value=True)
            nc.vector.tensor_reduce(tops[:, 2:3], b1[:], AX.X, ALU.max, apply_absolute_value=True).then_inc(tops_found, 1)
            dve.wait_ge(bounds_ready, 1)
            prep(nc.vector.scalar_tensor_tensor(bounds[:, 3:4], bounds[:, 0:1], float(D), bounds[:, 2:3],
                                                ALU.mult, ALU.add))
            prep(nc.vector.tensor_scalar(bounds[:], bounds[:], TINY, None, ALU.max))
            prep(nc.vector.tensor_scalar(powers[:].bitcast(I32), bounds[:].bitcast(I32), EXPONENT, None,
                                         ALU.bitwise_and))
            prep(nc.vector.reciprocal(inverses[:], powers[:]))
            nc.vector.tensor_scalar(up_scale[:], inverses[:, 0:1], TOP, None, ALU.mult)
            nc.vector.tensor_scalar(down_scale[:], inverses[:, 1:2], TOP, None, ALU.mult)
            nc.vector.tensor_scalar(hid_scale[:], inverses[:, 3:4], TOP, None, ALU.mult)
            nc.vector.tensor_scalar(up_back[:], powers[:, 0:1], 1.0 / (TOP * X_SCALE), None, ALU.mult)
            prep(nc.vector.tensor_scalar(back_root[:], powers[:, 1:2], 1.0 / (TOP * TOP), None, ALU.mult))
            nc.vector.tensor_tensor(down_back[:], back_root[:], powers[:, 3:4], ALU.mult)
            prep(nc.vector.tensor_scalar(b2_scaled[:], b2[:], hid_scale[:], down_scale[:], ALU.mult, ALU.mult))
            nc.vector.memset(spacer[:], 0.0).then_inc(scales_ready, 1)
            for k, (raw, parts, scale) in enumerate(((w1_raw, w1, up_scale), (w2_raw, w2, down_scale))):
                dve.wait_ge(high_ready, k + 1)
                nc.vector.scalar_tensor_tensor(parts[:, 1], raw, scale[:], parts[:, 0], ALU.mult,
                                               ALU.subtract).then_inc(low_ready, 1)
            nc.vector.memset(spacer[:], 0.0).then_inc(wb_ready, 1)
            dve.wait_ge(pads_set, 3)
            dve.wait_ge(wa_ready, 1)
            with dve.Fori(0, B) as b:
                attention(b)
                ffn(b, 0)
                scan_block(b)
                ffn(b, 1)


def shape_constants():
    inv_freq = (1.0 / np.float32(10000.0) ** (np.arange(0, HD, 2, dtype=np.float32) / np.float32(HD))).astype(np.float32)
    ang = np.arange(L, dtype=np.float32)[:, None] * inv_freq[None, :]
    cos = np.repeat(np.cos(ang), 2, axis=-1)
    sin = np.repeat(np.sin(ang), 2, axis=-1) * np.where(np.arange(HD) % 2 == 0, -1.0, 1.0)
    scale = np.array([1.0 / HD, 1.0])[:, None]

    def table(a):
        a = np.broadcast_to(a.reshape(TT, P, 1, HD), (TT, P, 2, HD)) * scale
        return a.transpose(1, 0, 2, 3).astype(np.float32)

    bf = mybir.dt.np(BF16)
    later = np.arange(P)[None, :] > np.arange(P)[:, None]
    pick = np.zeros((3, E, E, P), np.float32)
    for e in range(E):
        pick[:, e, e, :] = 1.0
    return {
        "cos": table(cos), "sin": table(sin), "ident": np.eye(P, dtype=np.float32),
        "neg_eye": (NEG_ROOT * np.eye(P)).astype(bf),
        "mask_qk": (-NEG_ROOT * later).astype(bf), "mask_kq": (-NEG_ROOT * later.T).astype(bf),
        "pick": pick.reshape(3 * E, E, P).astype(bf),
    }


def kernel(**inputs):
    import concourse.bacc as bacc
    from concourse.bass_utils import run_bass_kernel_spmd

    a = {k: np.asarray(v) for k, v in inputs.items()}
    w1 = np.concatenate([a["L0_ffn_W1"], a["L0_ffn_Ws1"][None]], 0)
    w2 = np.concatenate([a["L0_ffn_W2"], a["L0_ffn_Ws2"][None]], 0)
    b1 = np.concatenate([a["L0_ffn_b1"], a["L0_ffn_bs1"][None]], 0)
    b2 = np.concatenate([a["L0_ffn_b2"], a["L0_ffn_bs2"][None]], 0)
    arrays = {
        "x": a["L0_attn_a_x"],
        "wqkv": np.concatenate([a["L0_attn_a_Wq"].T, a["L0_attn_a_Wk"].T, a["L0_attn_a_Wv"].T], 1),
        "wo": a["L0_attn_a_Wo"].T,
        "bo": a["L0_attn_a_bo"][None],
        "w1": w1.transpose(2, 0, 1),
        "b1": b1.reshape(X * C, P).T,
        "w2": w2.reshape(X, D, C, P).transpose(3, 0, 2, 1),
        "b2": b2.T,
        "wg": a["L0_ffn_Wg"].T,
        "bg": a["L0_ffn_bg"][None],
        "bias": a["L0_ffn_bias"][None],
        "a_mat": a["L0_attn_b_A"].reshape(2, P, N).transpose(1, 0, 2),
        "bm": a["L0_attn_b_Bm"].reshape(2, P, N).transpose(1, 0, 2),
        "cm": a["L0_attn_b_Cm"],
        "dv": a["L0_attn_b_Dv"].reshape(2, P).T,
        "wdt": a["L0_attn_b_W_dt"].reshape(2, P).T,
        "conv": a["L0_attn_b_conv_w"].reshape(2, P, K).transpose(1, 0, 2),
        "win": a["L0_attn_b_W_in"].T,
        "wout": a["L0_attn_b_W_out"].T.reshape(2, P, D).transpose(1, 0, 2),
        **shape_constants(),
    }
    nc = bacc.Bacc("TRN2", target_bir_lowering=False, num_devices=1)
    args, given = [], {}
    for name, v in arrays.items():
        v = np.ascontiguousarray(v)
        given[f"in_{name}"] = v
        args.append(nc.dram_tensor(f"in_{name}", v.shape, mybir.dt.from_np(v.dtype), kind="ExternalInput").ap())
    out = nc.dram_tensor("out_x", (B, L, D), F32, kind="ExternalOutput").ap()
    hybrid_block_kernel(nc, *args, out)
    r = run_bass_kernel_spmd(nc, [given], core_ids=[0])
    return r.results[0]["out_x"]
```

```python
from contextlib import ExitStack

import numpy as np
import concourse.bass as bass
from concourse import mybir

ALU = mybir.AluOpType
ACT = mybir.ActivationFunctionType
AX = mybir.AxisListType
F32 = mybir.dt.float32
F16 = mybir.dt.float16
I32 = mybir.dt.int32
BF16 = mybir.dt.bfloat16

P = 128
D = 128
B = 4
L = 512
TT = L // P
H = 16
HD = D // H
G = 4
PAIRS = 2
W2 = 64
MAX_AT = 6 * HD
E = 8
X = E + 1
F = 512
C = F // P
N = 16
ED = 256
K = 3
STEP_AT = 32
EPS = 1e-5
NEG_ROOT = 100.0
FFNS = 2
HP = H // 2
MAX_UNITS = ((0, 1), (2,), (3,))
PROB_UNITS = ((0,), (1,), (2, 3))
UNITS = 2 * len(MAX_UNITS)
OW = 32
Q = 2 * PAIRS
PIECES = 8
PIECE = X * F // PIECES
PRODUCTS = [(0, 0), (1, 0), (0, 1)]
ORDER = [E] + list(range(E))
GATE_PAD = 16
PRE_LINKS = 8
CORE_LINKS = 21
FFN_LINKS = 7
SCAN_LINKS = 9
SLOTS = (1, 3, 4, 5)
X_SCALE = 2.0 ** 12
TOP = 2.0 ** 14
EXPONENT = 0x7F800000
TINY = 2.0 ** -60


def hybrid_block_kernel(nc, x_in, wqkv_in, wo_in, bo_in, w1_in, b1_in, w2_in, b2_in, wg_in, gate_rows_in,
                        a_in, bm_in, cm_in, dv_in, wdt_in, conv_in, win_in, win_rows_in, wout_in,
                        cos_in, sin_in, ident_dram, neg_eye_in, mask_qk_in, mask_kq_in, out):
    with ExitStack() as ctx:
        def sb(name, shape, dt=F32):
            return ctx.enter_context(nc.sbuf_tensor(name, shape, dt))

        def sem(name):
            return ctx.enter_context(nc.semaphore(name))

        ps = ctx.enter_context(nc.psum_tensor("ps", [P, 8, 512], F32))

        wqkv = sb("wqkv", [P, 3 * D])
        wo = sb("wo", [P, D])
        bo = sb("bo", [1, D])
        bo_all = sb("bo_all", [P, D])
        w1 = sb("w1", [P, 2, X, F], F16)
        b1 = sb("b1", [P, X * C])
        w2 = sb("w2", [P, 2, X, C, D], F16)
        b2 = sb("b2", [X, D])
        wg = sb("wg", [P, E])
        gate_rows = sb("gate_rows", [2, TT, E])
        a_mat = sb("a_mat", [P, 2, N])
        bm = sb("bm", [P, 2, N])
        cm = sb("cm", [N, ED])
        dv = sb("dv", [P, 2])
        wdt = sb("wdt", [P, 2])
        conv = sb("conv", [P, 2, K])
        win = sb("win", [P, 2 * ED])
        win_rows = sb("win_rows", [P, 2, D])
        wout = sb("wout", [P, 2, D])
        cos = sb("cos", [P, TT, 2, HD])
        sin = sb("sin", [P, TT, 2, HD])
        ident = sb("ident", [P, P])
        ident16 = sb("ident16", [P, P], BF16)
        neg_eye = sb("neg_eye", [P, P], BF16)
        mask_qk = sb("mask_qk", [P, P], BF16)
        mask_kq = sb("mask_kq", [P, P], BF16)
        ones = sb("ones", [2, P])
        minus_half = sb("minus_half", [P, TT])
        step_inner = sb("step_inner", [P, 2, STEP_AT + N])
        step_w = sb("step_w", [P, STEP_AT + N])
        wa = sb("wa", [N, 1])

        xin = sb("xin", [P, TT, D])
        x = sb("x", [P, TT, D])
        xout = sb("xout", [P, TT, D])
        stats = sb("stats", [P, TT, 6])
        mean_sum = sb("mean_sum", [P, TT])
        mean_dif = sb("mean_dif", [P, TT])
        sq_sum = sb("sq_sum", [P, TT])
        mean = sb("mean", [P, TT])
        spacer = sb("spacer", [P, 1])
        var_eps = sb("var_eps", [P, TT])
        rstd = sb("rstd", [P, TT])
        xn = sb("xn", [P, TT, D])
        xnT = sb("xnT", [P, L])

        rope_c = sb("rope_c", [P, TT, 2 * D])
        rope_s = sb("rope_s", [P, TT, 2 * D])
        qk_tok = sb("qk_tok", [P, 2, TT, H, W2], BF16)
        row_maxima = sb("row_maxima", [P, TT, H])
        max_rest = sb("max_rest", [P, TT, 2])
        v_tok = sb("v_tok", [P, TT, H, OW])
        xn_a = sb("xn_a", [P, TT, D])
        xnT_a = sb("xnT_a", [P, L])
        kT = sb("kT", [P, HP, L], BF16)
        q1T = sb("q1T", [P, HP, L], BF16)
        q2T = sb("q2T", [P, HP, L], BF16)
        probs = sb("probs", [P, 4, L])
        weighed = sb("weighed", [P, L])
        rec = sb("rec", [P, TT, Q])
        att = sb("att", [P, TT, D])
        attT = sb("attT", [P, L])

        score = sb("score", [P, TT, GATE_PAD])
        best = sb("best", [P, TT, 8])
        taken = sb("taken", [P, TT, 8])
        left = sb("left", [P, TT, GATE_PAD])
        route = sb("route", [P, TT, X])
        routeT = sb("routeT", [X, L])
        route_back = sb("route_back", [P, TT, X])
        x16 = sb("x16", [P, 2, L], F16)
        arena = sb("arena", [P, 12288])
        w1_raw = arena[:, 0:X * F].rearrange("p (e f) -> p e f", e=X)
        w2_raw = arena[:, X * F:2 * X * F].rearrange("p (e c d) -> p e c d", e=X, c=C)
        hid = arena[:, 4096:8192].rearrange("p (s c l) -> p s c l", s=2, c=C)
        hid16 = arena[:, 8192:12288].bitcast(F16).rearrange("p (s k c l) -> p s k c l", s=2, k=2, c=C)
        tops_part = sb("tops_part", [P, 2 * PIECES])
        tops = sb("tops", [P, 4])
        bounds = sb("bounds", [P, 4])
        powers = sb("powers", [P, 4])
        inverses = sb("inverses", [P, 4])
        up_scale = sb("up_scale", [P, 1])
        down_scale = sb("down_scale", [P, 1])
        hid_scale = sb("hid_scale", [P, 1])
        up_back = sb("up_back", [P, 1])
        down_back = sb("down_back", [P, 1])
        back_root = sb("back_root", [P, 1])
        weighted = sb("weighted", [P, 2, TT, D])

        xs, xcv = (arena[:, 4096 + 1024 * i:4096 + 1024 * (i + 1)].rearrange("p (c l) -> p c l", c=2)
                   for i in range(2))
        decay, step, u_in, state = (arena[0:N, 6144 + L * i:6144 + L * (i + 1)] for i in range(4))
        y, gate, diff, z = (arena[:, 1024 * i:1024 * (i + 1)].rearrange("p (c l) -> p c l", c=2) for i in range(4))

        consts_in = sem("consts_in")
        ffn_in = sem("ffn_in")
        scan_in = sem("scan_in")
        pads_set = sem("pads_set")
        POWER_SET, ZEROS_AND_ONES_SET, KEY_PADS_SET, STEP_WEIGHTS_SET, ALL_SET = range(1, 6)
        prep_step = sem("prep_step")
        pre_step = sem("pre_step")
        core_step = sem("core_step")
        ffn_step = sem("ffn_step")
        scan_step = sem("scan_step")
        tops_part_ready = sem("tops_part_ready")
        tops_found = sem("tops_found")
        bounds_ready = sem("bounds_ready")
        scales_ready = sem("scales_ready")
        high_ready = sem("high_ready")
        low_ready = sem("low_ready")
        x16_ready = sem("x16_ready")
        high16_ready = sem("high16_ready")
        own_high16_ready = sem("own_high16_ready")
        hid16_ready = sem("hid16_ready")
        xin_ready = sem("xin_ready")
        xin_free = sem("xin_free")
        ident_in = sem("ident_in")
        bo_made = sem("bo_made")
        bo_ready = sem("bo_ready")
        bias_added = sem("bias_added")
        out_stored = sem("out_stored")
        var_ready = sem("var_ready")
        rstd_ready = sem("rstd_ready")
        xn_ready = sem("xn_ready")
        xnT_made = sem("xnT_made")
        xnT_ready = sem("xnT_ready")
        v_made = sem("v_made")
        v_ready = sem("v_ready")
        qk_made = sem("qk_made")
        qk_read = sem("qk_read")
        ident16_ready = sem("ident16_ready")
        roped = sem("roped")
        kT_made = sem("kT_made")
        kT_ready = sem("kT_ready")
        q1T_made = sem("q1T_made")
        q1T_ready = sem("q1T_ready")
        score_made = sem("score_made")
        max_ready = sem("max_ready")
        max_split = sem("max_split")
        q2T_made = sem("q2T_made")
        q2T_ready = sem("q2T_ready")
        st_made = sem("st_made")
        exp_ready = sem("exp_ready")
        pv_made = sem("pv_made")
        weighed_ready = sem("weighed_ready")
        weighedT_made = sem("weighedT_made")
        att_ready = sem("att_ready")
        attT_made = sem("attT_made")
        attT_ready = sem("attT_ready")
        wo_made = sem("wo_made")
        gate_made = sem("gate_made")
        sig_ready = sem("sig_ready")
        route_ready = sem("route_ready")
        routeT_made = sem("routeT_made")
        routeT_ready = sem("routeT_ready")
        base_made = sem("base_made")
        base_added = sem("base_added")
        up_made = sem("up_made")
        gelu_ready = sem("gelu_ready")
        down_made = sem("down_made")
        down_read = sem("down_read")
        sum_ready = sem("sum_ready")
        wa_made = sem("wa_made")
        wa_ready = sem("wa_ready")
        wb_ready = sem("wb_ready")
        proj_made = sem("proj_made")
        xs_ready = sem("xs_ready")
        centre_ready = sem("centre_ready")
        dtu_made = sem("dtu_made")
        step_ready = sem("step_ready")
        state_ready = sem("state_ready")
        y_made = sem("y_made")
        y_ready = sem("y_ready")
        gate_ready = sem("gate_ready")
        z_ready = sem("z_ready")
        mo_made = sem("mo_made")
        residual_ready = sem("residual_ready")
        step_w_made = sem("step_w_made")
        step_w_ready = sem("step_w_ready")

        x_dram = x_in.rearrange("b (t p) d -> b p t d", p=P)
        out_dram = out.rearrange("b (t p) d -> b p t d", p=P)

        attn_loads = [(wqkv, wqkv_in), (cos, cos_in), (sin, sin_in), (wo, wo_in), (bo, bo_in),
                      (neg_eye, neg_eye_in), (mask_qk, mask_qk_in), (mask_kq, mask_kq_in)]
        ffn_loads = [(wg, wg_in), (gate_rows, gate_rows_in), (w1_raw, w1_in),
                     (b1, b1_in), (w2_raw, w2_in), (b2, b2_in)]
        scan_loads = [(a_mat, a_in), (bm, bm_in), (cm, cm_in), (dv, dv_in), (wdt, wdt_in), (conv, conv_in),
                      (win, win_in), (win_rows, win_rows_in), (wout, wout_in)]

        block = ctx.enter_context(nc.Block())

        def whole(t):
            return t[:] if not isinstance(t, bass.AP) else t

        def whole_row(t):
            return t.rearrange("p e f -> p (e f)" if len(t.shape) == 3 else "p e c d -> p (e c d)")

        def piece_of(t, piece):
            return whole_row(t)[:, piece * PIECE:(piece + 1) * PIECE]

        MISC = 0
        GATE = 1
        S_BANKS = (1, 0)
        S_BANKS_FIRST = (3, 2)
        S_BANKS_ALONE = (1, 4)
        ST_BANKS = (2, 3)
        ST_BANKS_ALONE = (2, 3, 5)
        UP_BANKS = (4, 5)
        DOWN_BANKS = (6, 3)
        WEIGHED_BANKS = (7,)
        WEIGHED_ALONE = (7, 6)
        QK_BANKS = (1, 2)
        V_BANK = 7
        Y_BANKS = (7, 6)
        TURN_BANKS = (0, 1, 2, 7)

        @block.sync
        def _(sp):
            sp.dma_start(xin[:], x_dram[0]).then_inc(xin_ready, 16)
            sp.dma_start(ident[:], ident_dram).then_inc(ident_in, 16)
            for dst, src in attn_loads:
                sp.dma_start(whole(dst), src).then_inc(consts_in, 16)
            for dst, src in ffn_loads:
                sp.dma_start(whole(dst), src).then_inc(ffn_in, 16)
            for dst, src in scan_loads:
                sp.dma_start(whole(dst), src).then_inc(scan_in, 16)

            def store(b, where):
                sp.wait_ge(sum_ready, (b + 1) * FFNS * X)
                sp.dma_start(where, xout[:]).then_inc(out_stored, 16)

            def of_batch(dram, b):
                return dram[bass.ds(b, 1)].rearrange("o p t d -> (o p) t d")

            with sp.Fori(0, B - 1) as b:
                sp.wait_ge(xin_free, b + 1)
                sp.dma_start(xin[:], of_batch(x_dram, b + 1)).then_inc(xin_ready, 16)
                store(b, of_batch(out_dram, b))
            store(B - 1, out_dram[B - 1])
            sp.wait_ge(out_stored, 16 * B + 16)

        @block.gpsimd
        def _(pool):
            def inverse_root(n):
                pool.wait_ge(var_ready, n + 1)
                nc.gpsimd.tensor_tensor(rstd[:], var_eps[:], minus_half[:], ALU.pow).then_inc(rstd_ready, 1)

            nc.gpsimd.memset(minus_half[:], -0.5).then_inc(pads_set, 1)
            nc.gpsimd.memset(ones[:], 1.0)
            nc.gpsimd.memset(qk_tok[:].bitcast(I32), 0).then_inc(pads_set, 1)
            pool.wait_ge(pads_set, POWER_SET)
            inverse_root(0)
            pool.wait_ge(pads_set, ZEROS_AND_ONES_SET)
            nc.gpsimd.memset(qk_tok[:, 1, :, :, MAX_AT:MAX_AT + 2], -1.0).then_inc(pads_set, 1)
            nc.gpsimd.memset(v_tok[:], 0.0)
            nc.gpsimd.memset(route[:], 1.0)
            nc.gpsimd.memset(score[:], -1.0)
            nc.gpsimd.memset(taken[:], -1.0).then_inc(out_stored, 16)
            nc.gpsimd.memset(step_inner[:, :, 0:STEP_AT], 0.0)
            nc.gpsimd.memset(step_inner[:, :, STEP_AT:], 1.0 / ED).then_inc(pads_set, 1)
            pool.wait_ge(pads_set, STEP_WEIGHTS_SET)
            nc.gpsimd.memset(v_tok[:, :, :, HD:HD + 1], 1.0).then_inc(pads_set, 1)

            def add_bias(a, n):
                pool.wait_ge(xn_ready, n * TT + TT)
                nc.gpsimd.tensor_tensor(xin[:], xin[:], bo_all[:].unsqueeze(1).broadcast_to([P, TT, D]),
                                        ALU.add).then_inc(bias_added, 1)

            pool.wait_ge(bo_ready, 1)
            add_bias(0, 0)
            pool.wait_ge(tops_found, 1)
            nc.gpsimd.partition_all_reduce(bounds[:, 0:3], tops[:, 0:3], P,
                                           bass.bass_isa.ReduceOp.max).then_inc(bounds_ready, 1)

            def ffn(b, r, n, pre_n=None):
                f = b * FFNS + r
                inverse_root(n)
                for i in range(X - 1):
                    if i == 0:
                        pool.wait_ge(base_added, f + 1)
                    else:
                        pool.wait_ge(sum_ready, f * X + i)
                    pool.wait_ge(down_read, f * X + i + 1)
                    nc.gpsimd.tensor_tensor(x[:], x[:], weighted[:, i % 2], ALU.add).then_inc(sum_ready, 1)
                    if i == 0 and pre_n is not None:
                        inverse_root(pre_n)
                    if i == 2 and pre_n is not None:
                        add_bias(b + 1, pre_n)

            def scan_block(b, n):
                inverse_root(n)
                pool.wait_ge(xn_ready, n * TT + TT)
                nc.gpsimd.tensor_tensor(x[:], x[:], xn[:], ALU.add).then_inc(residual_ready, 1)

            with pool.Fori(0, B - 1) as b:
                ffn(b, 0, 4 * b + 1, 4 * b + 2)
                scan_block(b, 4 * b + 3)
                ffn(b, 1, 4 * b + 4)
            last = B - 1
            ffn(last, 0, 4 * last + 1)
            scan_block(last, 4 * last + 2)
            ffn(last, 1, 4 * last + 3)

        @block.scalar
        def _(act):
            def norm_T(n):
                act.wait_ge(xnT_made, n + 1)
                nc.scalar.copy(xnT[:], ps[:, MISC, :]).then_inc(xnT_ready, 1)

            def pre_tokens(n):
                act.wait_ge(xnT_made, n + 1)
                nc.scalar.copy(xnT_a[:], ps[:, V_BANK, :]).then_inc(xnT_ready, 1)

            def pre_values(a):
                act.wait_ge(v_made, a + 1)
                nc.scalar.copy(v_tok[:, :, :, 0:HD],
                               ps[:, V_BANK, :].rearrange("p (t h d) -> p t h d", t=TT, h=H)).then_inc(v_ready, 1)

            def pre_keys(a, groups=range(G)):
                for g in groups:
                    act.wait_ge(kT_made, a * G + g + 1)
                    nc.scalar.copy(kT[:, 2 * g:2 * g + 2, :].rearrange("p a l -> p (a l)"),
                                   ps[:, TURN_BANKS[2 * g % 4], :].bitcast(BF16)).then_inc(kT_ready, 1)

            def queries_with_max(a, p):
                act.wait_ge(q2T_made, a * HP + p + 1)
                nc.scalar.copy(q2T[:, p, :], ps[:, MISC, 0:L // 2].bitcast(BF16)).then_inc(q2T_ready, 1)

            def exps(a, p, units=range(UNITS), banks=ST_BANKS):
                for u in units:
                    m = p * UNITS + u
                    n = sum(L - P * j for j in PROB_UNITS[u // 2])
                    act.wait_ge(st_made, a * HP * UNITS + m + 1)
                    if m >= 4:
                        act.wait_ge(pv_made, a * HP * UNITS + m - 3)
                    nc.scalar.activation(probs[:, m % 4, 0:n], ps[:, banks[m % len(banks)], 0:n],
                                         ACT.Exp).then_inc(exp_ready, 1)

            def take_weighed(a, g, banks=WEIGHED_BANKS):
                act.wait_ge(pv_made, (a * HP + 2 * g + 2) * UNITS)
                nc.scalar.copy(weighed[:], ps[:, banks[g % len(banks)], :]).then_inc(weighed_ready, 1)

            def attention_post(a):
                act.wait_ge(attT_made, a + 1)
                nc.scalar.copy(attT[:], ps[:, 4, :]).then_inc(attT_ready, 1)

            def ffn(b, r, n, a=None, pre_n=None):
                f = b * FFNS + r
                norm_T(n)
                act.wait_ge(gate_made, f + 1)
                act.wait_ge(pads_set, ALL_SET)
                nc.scalar.activation(score[:, :, 0:E], ps[:, GATE, 0:TT * E].rearrange("p (t e) -> p t e", t=TT),
                                     ACT.Sigmoid).then_inc(sig_ready, 1)

                def gelu(i, c):
                    n = i * C + c
                    act.wait_ge(up_made, f * X * C + n + 1)
                    if i >= 2 and c == 0:
                        act.wait_ge(hid16_ready, f * X * 2 + 2 * i - 2)
                    nc.scalar.activation(hid[:, i % 2, c, :], ps[:, UP_BANKS[n % 2], :], ACT.Gelu,
                                         bias=b1[:, ORDER[i] * C + c:ORDER[i] * C + c + 1],
                                         scale=up_back[:]).then_inc(gelu_ready, 1)

                def take_high(i, half):
                    act.wait_ge(gelu_ready, f * X * C + i * C + 2 * half + 2)
                    if i >= 2 and half == 0:
                        act.wait_ge(down_made, f * X + i - 1)
                    two = slice(2 * half, 2 * half + 2)
                    nc.scalar.activation(hid16[:, i % 2, 0, two], hid[:, i % 2, two], ACT.Identity,
                                         scale=hid_scale[:]).then_inc(high16_ready, 1)

                def gelus(i, soft):
                    for c in range(C):
                        gelu(i, c)
                        if c == 1 and soft and i >= 1:
                            queries_with_max(a, i - 1)
                            if i in (3, 5, 7):
                                take_weighed(a, i // 2 - 1)
                        if c == 1 and a is not None and r == 0:
                            if i == 3:
                                pre_tokens(pre_n)
                            if i == 6:
                                pre_values(a)
                        if c >= 2 and not soft and 0 < i < X - 1:
                            take_high(i, c - 2)

                soft = a is not None and r == 1

                def take_route():
                    act.wait_ge(routeT_made, f + 1)
                    nc.scalar.copy(routeT[:], ps[0:X, MISC, :]).then_inc(routeT_ready, 1)

                gelus(0, soft)
                if soft:
                    take_route()
                for i in range(X):
                    if i + 1 < X:
                        gelus(i + 1, soft)
                    if i == 0 and not soft:
                        take_route()
                    if soft:
                        if i < HP:
                            exps(a, i)
                        else:
                            take_weighed(a, G - 1)
                    if a is not None and r == 0 and i >= HP - 1:
                        pre_keys(a, ((0, 1), (2, 3))[i - HP + 1])

            def scan_block(b, n):
                norm_T(n)
                act.wait_ge(dtu_made, b + 1)
                nc.scalar.copy(step, ps[STEP_AT:STEP_AT + N, 5, :]).then_inc(step_ready, 1)
                for c in range(2):
                    act.wait_ge(proj_made, b * 4 + c + 1)
                    nc.scalar.copy(xs[:, c, :], ps[:, 3 + c, :]).then_inc(xs_ready, 1)
                for c in range(2):
                    act.wait_ge(proj_made, b * 4 + c + 3)
                    nc.scalar.activation(xcv[:, c, :], ps[:, 1 + c, :], ACT.Identity,
                                         scale=conv[:, c, 1:2]).then_inc(centre_ready, 1)
                for c in range(2):
                    act.wait_ge(y_ready, b * 2 + c + 1)
                    nc.scalar.activation(gate[:, c, :], y[:, c, :], ACT.Sigmoid).then_inc(gate_ready, 1)

            def take_high_weights(k, piece):
                raw, parts, scale = ((w1_raw, w1, up_scale), (w2_raw, w2, down_scale))[k]
                if k == 0 and piece == 0:
                    act.wait_ge(scales_ready, 1)
                raw, high = piece_of(raw, piece), piece_of(parts[:, 0], piece)
                nc.scalar.activation(high, raw, ACT.Identity, scale=scale[:]).then_inc(high_ready, 1)

            pre_tokens(0)
            act.wait_ge(bo_made, 1)
            nc.scalar.copy(bo_all[:], ps[:, 0, 0:D]).then_inc(bo_ready, 1)
            act.wait_ge(pads_set, ALL_SET)
            pre_values(0)
            pre_keys(0)
            for i in range(1, HP + 1):
                queries_with_max(0, i - 1)
                if i in (3, 5, 7):
                    take_weighed(0, i // 2 - 1, WEIGHED_ALONE)
                for u in range(UNITS):
                    exps(0, i - 1, (u,), ST_BANKS_ALONE)
                    if i >= 5 and u in SLOTS:
                        n = 4 * (i - 5) + SLOTS.index(u)
                        take_high_weights(n // PIECES, n % PIECES)
            act.wait_ge(wa_made, 1)
            nc.scalar.copy(wa[:], ps[0:N, S_BANKS_ALONE[1], 0:1]).then_inc(wa_ready, 1)
            act.wait_ge(step_w_made, 1)
            nc.scalar.copy(step_w[:], ps[:, S_BANKS_ALONE[0], 0:STEP_AT + N]).then_inc(step_w_ready, 1)
            take_weighed(0, G - 1, WEIGHED_ALONE)
            attention_post(0)
            with act.Fori(0, B - 1) as b:
                ffn(b, 0, 4 * b + 1, b + 1, 4 * b + 2)
                scan_block(b, 4 * b + 3)
                ffn(b, 1, 4 * b + 4, b + 1)
                attention_post(b + 1)
            last = B - 1
            ffn(last, 0, 4 * last + 1)
            scan_block(last, 4 * last + 2)
            ffn(last, 1, 4 * last + 3)

        @block.tensor
        def _(pe):
            def norm_T(n, src, bank):
                for t in range(TT):
                    pe.wait_ge(xn_ready, n * TT + t + 1)
                    mm = pe.transpose(ps[:, bank, t * P:(t + 1) * P], src[:, t, :], ident[:])
                mm.then_inc(xnT_made, 1)

            def keep_clock(count, bank):
                for _ in range(count):
                    pe.matmul(ps[:, bank, :], w1[:, 0, 0, 0:P], w1[:, 0, 0, :], start=True, stop=True)

            def pre_qk(a, n, t0):
                pe.wait_ge(xnT_ready, n + 1)
                for t in (t0, t0 + 1):
                    o = (t % 2) * 2 * D
                    pe.matmul(ps[:, QK_BANKS[t // 2], o:o + 2 * D], xnT_a[:, t * P:(t + 1) * P], wqkv[:, 0:2 * D],
                              start=True, stop=True).then_inc(qk_made, 1)

            def pre_values(a):
                for t in range(TT):
                    mm = pe.matmul(ps[:, V_BANK, t * D:(t + 1) * D], xnT_a[:, t * P:(t + 1) * P],
                                   wqkv[:, 2 * D:3 * D], start=True, stop=True)
                mm.then_inc(v_made, 1)

            def pair_T(to, k, p):
                for t in range(TT):
                    mm = pe.transpose(to[:, t * P:(t + 1) * P],
                                      qk_tok[:, k, t, 2 * p:2 * p + 2, :].rearrange("p h w -> p (h w)"), ident16[:])
                return mm

            def pre_T(a, groups=range(G)):
                for g in groups:
                    if g == 0:
                        pe.wait_ge(roped, a + 1)
                        pe.wait_ge(v_ready, a + 1)
                    for k, made, read in ((1, kT_made, kT_ready), (0, q1T_made, q1T_ready)):
                        if g >= 2:
                            pe.wait_ge(read, a * G + g - 1)
                        bank = ps[:, TURN_BANKS[(2 * g + 1 - k) % 4], :].bitcast(BF16)
                        bank = bank.rearrange("p (a l) -> p a l", a=PAIRS)
                        for x in range(PAIRS):
                            mm = pair_T(bank[:, x, :], k, 2 * g + x)
                        mm.then_inc(made, 1)

            def scores(a, p, u, alone=False, banks=None):
                n, h, o = p * UNITS + u, u % 2, 0
                if u == 1 and p >= 1 and not alone:
                    pe.wait_ge(q2T_ready, a * HP + p)
                elif n >= 2:
                    pe.wait_ge(max_ready, a * HP * UNITS + n - 1)
                rows = slice(W2 * h, W2 * h + MAX_AT)
                for t in MAX_UNITS[u // 2]:
                    keys = P * (t + 1)
                    to = ps[:, (banks or (S_BANKS_ALONE if alone else S_BANKS))[n % 2], o:o + keys]
                    pe.matmul(to, q1T[rows, p, t * P:(t + 1) * P], kT[rows, p, 0:keys], start=True, stop=False)
                    mm = pe.matmul(to[:, keys - P:keys], neg_eye[:], mask_qk[:], start=False, stop=True)
                    o += keys
                mm.then_inc(score_made, 1)

            def queries_with_max(a, p, alone=False):
                pe.wait_ge(max_split, a * HP + p + 1)
                if p >= 1 and not alone:
                    pe.wait_ge(max_ready, (a * HP + p + 1) * UNITS)
                pair_T(ps[:, MISC, 0:L // 2].bitcast(BF16), 0, p).then_inc(q2T_made, 1)

            def scores_T(a, p, u, banks=ST_BANKS):
                m, h, o = p * UNITS + u, u % 2, 0
                if u == 0:
                    pe.wait_ge(q2T_ready, a * HP + p + 1)
                if m >= len(banks):
                    pe.wait_ge(exp_ready, a * HP * UNITS + m + 1 - len(banks))
                rows = slice(W2 * h, W2 * h + W2)
                for j in PROB_UNITS[u // 2]:
                    n = L - P * j
                    to = ps[:, banks[m % len(banks)], o:o + n]
                    pe.matmul(to, kT[rows, p, j * P:(j + 1) * P], q2T[rows, p, j * P:L], start=True, stop=False)
                    mm = pe.matmul(to[:, 0:P], neg_eye[:], mask_kq[:], start=False, stop=True)
                    o += n
                mm.then_inc(st_made, 1)

            def weigh_values(a, p, u, banks=WEIGHED_BANKS):
                m, h, at = p * UNITS + u, u % 2, 0
                if u == 0 and p % 2 == 0 and p >= 2 * len(banks):
                    pe.wait_ge(att_ready, a * G + p // 2 + 1 - len(banks))
                pe.wait_ge(exp_ready, a * HP * UNITS + m + 1)
                quadrant, bank = OW * (2 * (p % 2) + h), banks[p // 2 % len(banks)]
                for j in PROB_UNITS[u // 2]:
                    n = L - P * j
                    mm = pe.matmul(ps[quadrant:quadrant + OW, bank, j * P:L], v_tok[:, j, 2 * p + h, :],
                                   probs[:, m % 4, at:at + n], start=(j == 0), stop=(j == TT - 1))
                    at += n
                mm.then_inc(pv_made, 1)

            def weighed_T(a, g, banks=WEIGHED_BANKS):
                pe.wait_ge(weighed_ready, a * G + g + 1)
                for t in range(TT):
                    mm = pe.transpose(ps[:, banks[g % len(banks)], t * P:(t + 1) * P],
                                      weighed[:, t * P:(t + 1) * P], ident[:])
                mm.then_inc(weighedT_made, 1)

            def softmax_end(a, p, banks=WEIGHED_BANKS):
                weigh_values(a, p, UNITS - 2, banks)
                weigh_values(a, p, UNITS - 1, banks)

            def softmax_alone(a, i):
                if i < HP:
                    scores(a, i, 0, True)
                if i >= 1:
                    queries_with_max(a, i - 1, True)
                if i < HP:
                    scores(a, i, 1, True)
                if i >= 2:
                    softmax_end(a, i - 2, WEIGHED_ALONE)
                if i >= 1:
                    for u in range(3):
                        scores_T(a, i - 1, u, ST_BANKS_ALONE)
                for u in range(2, UNITS):
                    if i < HP:
                        scores(a, i, u, True)
                    if u == 3 and i in (3, 5, 7):
                        weighed_T(a, i // 2 - 1, WEIGHED_ALONE)
                    if i >= 1 and u >= 3:
                        weigh_values(a, i - 1, u - 3, WEIGHED_ALONE)
                        scores_T(a, i - 1, u, ST_BANKS_ALONE)
                if i >= 1:
                    weigh_values(a, i - 1, 3, WEIGHED_ALONE)

            def attention_post(a):
                pe.wait_ge(att_ready, a * G + G)
                for t in range(TT):
                    mm = pe.transpose(ps[:, 4, t * P:(t + 1) * P], att[:, t, :], ident[:])
                mm.then_inc(attT_made, 1)
                pe.wait_ge(attT_ready, a + 1)
                for t in range(TT):
                    mm = pe.matmul(ps[:, 5, t * D:(t + 1) * D], attT[:, t * P:(t + 1) * P], wo[:], start=True,
                                   stop=True)
                mm.then_inc(wo_made, 1)
                keep_clock(22, ST_BANKS[1])

            def ffn(b, r, n, a=None, pre_n=None):
                f = b * FFNS + r
                soft = a is not None and r == 1
                down_turns = 1 if soft else 2
                norm_T(n, xn, MISC)
                pe.wait_ge(xnT_ready, n + 1)
                pe.matmul(ps[:, GATE, 0:TT * E], ones[:], gate_rows[:].rearrange("r t e -> r (t e)"), start=True,
                          stop=False, skip_group_check=True)
                for t in range(TT):
                    mm = pe.matmul(ps[:, GATE, t * E:(t + 1) * E], xnT[:, t * P:(t + 1) * P], wg[:], start=False,
                                   stop=True, skip_group_check=True)
                mm.then_inc(gate_made, 1)
                if soft:
                    scores(a, 0, 4, banks=S_BANKS_FIRST)
                    scores(a, 0, 5, banks=S_BANKS_FIRST)

                def bias_outputs():
                    pe.wait_ge(routeT_ready, f + 1)
                    for t in range(TT):
                        mm = pe.matmul(ps[:, MISC, t * D:(t + 1) * D], routeT[:, t * P:(t + 1) * P], b2[:],
                                       start=True, stop=True)
                    mm.then_inc(base_made, 1)

                def up(i, c):
                    n = i * C + c
                    if n >= 2:
                        pe.wait_ge(gelu_ready, f * X * C + n - 1)
                    for k, (w, v) in enumerate(PRODUCTS):
                        mm = pe.matmul(ps[:, UP_BANKS[n % 2], :], w1[:, w, ORDER[i], c * P:(c + 1) * P], x16[:, v, :],
                                       start=(k == 0), stop=(k == 2))
                    mm.then_inc(up_made, 1)

                def down(i, c):
                    if c == 0 and i >= down_turns:
                        pe.wait_ge(down_read, f * X + i + 1 - down_turns)
                    if c % 2 == 0:
                        pe.wait_ge(hid16_ready, f * X * 2 + 2 * i + c // 2 + 1)
                    for k, (w, v) in enumerate(PRODUCTS):
                        for t in range(TT):
                            mm = pe.matmul(ps[:, DOWN_BANKS[i % down_turns], t * D:(t + 1) * D],
                                           hid16[:, i % 2, v, c, t * P:(t + 1) * P],
                                           w2[:, w, ORDER[i], c, :], start=(c == 0 and k == 0 and t == 0),
                                           stop=(c == C - 1 and k == 2), skip_group_check=True)
                    if c == C - 1:
                        mm.then_inc(down_made, 1)

                pe.wait_ge(x16_ready, f + 1)
                for c in range(C):
                    up(0, c)
                up(1, 0)
                up(1, 1)
                pe.wait_ge(route_ready, f + 1)
                for t in range(TT):
                    mm = pe.transpose(ps[0:X, MISC, t * P:(t + 1) * P], route[:, t, :], ident[:])
                mm.then_inc(routeT_made, 1)
                for i in range(X):
                    weigh, maxima = soft and i < HP, soft and i + 1 < HP
                    if soft and i >= 1:
                        softmax_end(a, i - 1)
                    if maxima:
                        scores(a, i + 1, 0)
                    if soft:
                        down(i, 0)
                        if i == 0:
                            bias_outputs()
                            pe.wait_ge(base_added, f + 1)
                    if weigh:
                        queries_with_max(a, i)
                    if i + 1 < X:
                        up(i + 1, 2)
                    if not soft:
                        down(i, 0)
                    if i + 1 < X:
                        up(i + 1, 3)
                    if maxima:
                        scores(a, i + 1, 1)
                    down(i, 1)
                    if soft and i in (2, 4, 6, 8):
                        weighed_T(a, i // 2 - 1)
                    if maxima:
                        scores(a, i + 1, 2)
                    if weigh:
                        scores_T(a, i, 0)
                        scores_T(a, i, 1)
                    if not soft and i + 2 < X:
                        up(i + 2, 0)
                    down(i, 2)
                    if not soft and i + 2 < X:
                        up(i + 2, 1)
                    if maxima:
                        scores(a, i + 1, 3)
                    if weigh:
                        weigh_values(a, i, 0)
                        scores_T(a, i, 2)
                        weigh_values(a, i, 1)
                        scores_T(a, i, 3)
                    if a is not None and r == 0 and i >= HP - 1:
                        pre_T(a, ((0,), (2,))[i - HP + 1])
                    down(i, 3)
                    if weigh:
                        weigh_values(a, i, 2)
                        scores_T(a, i, 4)
                    if maxima:
                        scores(a, i + 1, 4)
                    if soft and i + 2 < X:
                        up(i + 2, 0)
                    if weigh:
                        weigh_values(a, i, 3)
                        scores_T(a, i, 5)
                    if maxima:
                        scores(a, i + 1, 5)
                    if soft and i + 2 < X:
                        up(i + 2, 1)
                    if i == 0 and not soft:
                        bias_outputs()
                    if a is not None and r == 0:
                        if i == 1:
                            norm_T(pre_n, xn_a, V_BANK)
                        if i == 2:
                            pre_qk(a, pre_n, 0)
                            pre_qk(a, pre_n, 2)
                        if i == 4:
                            pre_values(a)
                        if i == HP - 1:
                            pre_T(a, (1,))
                        if i == HP:
                            pre_T(a, (3,))
                if r == 0:
                    keep_clock(18, UP_BANKS[0])

            def scan_block(b, n, a=None):
                if a is not None:
                    pe.wait_ge(kT_ready, a * G + 3)
                norm_T(n, xn, MISC)
                pe.wait_ge(xnT_ready, n + 1)
                pe.matmul(ps[0:STEP_AT + N, 5, :], step_w[:], xnT[:], start=True, stop=True).then_inc(dtu_made, 1)
                for k in (2, 3, 0, 1):
                    if a is not None and k == 0:
                        pe.wait_ge(kT_ready, a * G + G)
                        pe.wait_ge(q1T_ready, a * G + G)
                    pe.matmul(ps[:, 1 + k, :], win[:, k * P:(k + 1) * P], xnT[:], start=True,
                              stop=True).then_inc(proj_made, 1)
                pe.wait_ge(state_ready, b + 1)
                for c in range(2):
                    pe.matmul(ps[:, Y_BANKS[c], :], cm[:, c * P:(c + 1) * P], state, start=True,
                              stop=True).then_inc(y_made, 1)
                if a is not None:
                    pe.wait_ge(xs_ready, b * 2 + 1)
                    scores(a, 0, 0, banks=S_BANKS_FIRST)
                    pe.wait_ge(y_ready, b * 2 + 1)
                    scores(a, 0, 1, banks=S_BANKS_FIRST)
                pe.wait_ge(xs_ready, b * 2 + 2)
                keep_clock(10, 4)
                for c in range(2):
                    pe.wait_ge(z_ready, b * 2 + c + 1)
                    for t in range(TT):
                        mm = pe.matmul(ps[:, 1, t * D:(t + 1) * D], z[:, c, t * P:(t + 1) * P], wout[:, c, :],
                                       start=(c == 0 and t == 0), stop=(c == 1), skip_group_check=True)
                mm.then_inc(mo_made, 1)
                if a is not None:
                    scores(a, 0, 2, banks=S_BANKS_FIRST)
                    scores(a, 0, 3, banks=S_BANKS_FIRST)
                keep_clock(16, 4)

            pe.wait_ge(ident_in, 16)
            norm_T(0, xn_a, V_BANK)
            pe.wait_ge(consts_in, 16 * len(attn_loads))
            pe.wait_ge(pads_set, ZEROS_AND_ONES_SET)
            pe.matmul(ps[:, 0, 0:D], ones[0:1, :], bo[:], start=True, stop=True).then_inc(bo_made, 1)
            pre_qk(0, 0, 0)
            pre_qk(0, 0, 2)
            pre_values(0)
            pe.wait_ge(ident16_ready, 1)
            pre_T(0)
            pe.wait_ge(pads_set, ALL_SET)
            pe.wait_ge(kT_ready, G)
            pe.wait_ge(q1T_ready, G)
            for i in range(HP + 1):
                softmax_alone(0, i)
            pe.wait_ge(scan_in, 16 * len(scan_loads))
            for c in range(2):
                mm = pe.matmul(ps[0:N, S_BANKS_ALONE[1], 0:1], a_mat[:, c, :], wdt[:, c:c + 1], start=(c == 0),
                               stop=(c == 1))
            mm.then_inc(wa_made, 1)
            pe.wait_ge(wb_ready, 1)
            for c in range(2):
                mm = pe.matmul(ps[:, S_BANKS_ALONE[0], 0:STEP_AT + N], win_rows[:, c, :], step_inner[:, c, :],
                               start=(c == 0), stop=(c == 1))
            mm.then_inc(step_w_made, 1)
            softmax_end(0, HP - 1, WEIGHED_ALONE)
            weighed_T(0, G - 1, WEIGHED_ALONE)
            pe.wait_ge(wa_ready, 1)
            pe.wait_ge(step_w_ready, 1)
            pe.wait_ge(ffn_in, 16 * len(ffn_loads))
            pe.wait_ge(low_ready, 2 * PIECES)
            attention_post(0)
            with pe.Fori(0, B - 1) as b:
                ffn(b, 0, 4 * b + 1, b + 1, 4 * b + 2)
                scan_block(b, 4 * b + 3, b + 1)
                ffn(b, 1, 4 * b + 4, b + 1)
                attention_post(b + 1)
            last = B - 1
            ffn(last, 0, 4 * last + 1)
            scan_block(last, 4 * last + 2)
            ffn(last, 1, 4 * last + 3)

        @block.vector
        def _(dve):
            class Links:
                def __init__(self, semaphore, per_stage):
                    self.semaphore, self.per_stage, self.n = semaphore, per_stage, 0

                def __call__(self, stage, ins):
                    self.n += 1
                    ins.then_inc(self.semaphore, 1)
                    dve.wait_ge(self.semaphore, stage * self.per_stage + self.n)

                def end(self):
                    assert self.n == self.per_stage, self.n
                    self.n = 0

            pre_link = Links(pre_step, PRE_LINKS)
            core_link = Links(core_step, CORE_LINKS)
            ffn_link = Links(ffn_step, FFN_LINKS)
            scan_link = Links(scan_step, SCAN_LINKS)

            def norm_stats(n, src, link, stage):
                for t in range(TT):
                    ins = nc.vector.bn_stats(stats[:, t, :], src[:, t, :])
                link(stage, ins)
                mean_e, sq_e, mean_o, sq_o = (stats[:, :, i] for i in (1, 2, 4, 5))
                nc.vector.tensor_tensor(mean_sum[:], mean_e, mean_o, ALU.add)
                nc.vector.tensor_tensor(mean_dif[:], mean_e, mean_o, ALU.subtract)
                link(stage, nc.vector.scalar_tensor_tensor(sq_sum[:], sq_e, D * EPS, sq_o, ALU.add, ALU.add))
                nc.vector.tensor_scalar(mean[:], mean_sum[:], 0.5, None, ALU.mult)
                link(stage, nc.vector.scalar_tensor_tensor(mean_dif[:], mean_dif[:], 0.25, mean_dif[:],
                                                           ALU.mult, ALU.mult))
                nc.vector.scalar_tensor_tensor(var_eps[:], sq_sum[:], 1.0 / D, mean_dif[:], ALU.mult,
                                               ALU.add).then_inc(var_ready, 1)

            def norm_apply(n, src, to):
                dve.wait_ge(rstd_ready, n + 1)
                for t in range(TT):
                    nc.vector.tensor_scalar(to[:, t, :], src[:, t, :], mean[:, t:t + 1], rstd[:, t:t + 1],
                                            ALU.subtract, ALU.mult).then_inc(xn_ready, 1)

            def rotate(a, t):
                dve.wait_ge(qk_made, a * TT + t // 2 * 2 + 2)
                qk = ps[:, QK_BANKS[t // 2], (t % 2) * 2 * D:(t % 2 + 1) * 2 * D]

                def by_head(x):
                    return x.rearrange("p (k h d) -> p k h d", k=2, h=H)

                def all_heads(table, part):
                    x = table[:, t, :, part]
                    return x.unsqueeze(2).broadcast_to([P, 2, H, x.shape[2]])

                even, odd = slice(0, HD, 2), slice(1, HD, 2)
                nc.vector.tensor_tensor(by_head(rope_c[:, t, :]), by_head(qk), all_heads(cos, slice(0, HD)), ALU.mult)
                for to, of in ((even, odd), (odd, even)):
                    ins = nc.vector.tensor_tensor(by_head(rope_s[:, t, :])[:, :, :, to], by_head(qk)[:, :, :, of],
                                                  all_heads(sin, to), ALU.mult)
                ins.then_inc(qk_read, 1)

            qk32 = rope_c[:].rearrange("p t (k h d) -> p k t h d", k=2, h=H)
            rest = rope_s[:].rearrange("p t (k h d) -> p k t h d", k=2, h=H)

            def slot(k, n):
                return qk_tok[:, k, :, :, n * HD:(n + 1) * HD]

            def rotated(a):
                dve.wait_ge(qk_read, a * TT + TT)
                pre_link(a, nc.vector.tensor_tensor(rope_c[:], rope_c[:], rope_s[:], ALU.add))

            def take_high(a):
                for k in range(2):
                    ins = nc.vector.tensor_copy(slot(k, 0), qk32[:, k])
                pre_link(a, ins)
                nc.vector.tensor_copy(slot(0, 2), slot(0, 0))
                nc.vector.tensor_copy(slot(1, 3), slot(1, 0))

            def less_high(a):
                for k in range(2):
                    ins = nc.vector.tensor_tensor(rest[:, k], qk32[:, k], slot(k, 0), ALU.subtract)
                pre_link(a, ins)

            def take_middle(a):
                for k in range(2):
                    ins = nc.vector.tensor_copy(slot(k, 1), rest[:, k])
                pre_link(a, ins)
                nc.vector.tensor_copy(slot(0, 4), slot(0, 0))
                nc.vector.tensor_copy(slot(1, 5), slot(1, 0))

            def less_middle(a):
                for k in range(2):
                    ins = nc.vector.tensor_tensor(rest[:, k], rest[:, k], slot(k, 1), ALU.subtract)
                pre_link(a, ins)

            def take_low(a):
                nc.vector.tensor_copy(slot(0, 3), slot(0, 1))
                nc.vector.tensor_copy(slot(1, 2), slot(1, 1))
                nc.vector.tensor_copy(slot(0, 5), rest[:, 0])
                nc.vector.tensor_copy(slot(1, 4), rest[:, 1]).then_inc(roped, 1)
                pre_link.end()

            def pre_queries(a, groups=range(G)):
                for g in groups:
                    dve.wait_ge(q1T_made, a * G + g + 1)
                    nc.vector.tensor_copy(q1T[:, 2 * g:2 * g + 2, :].rearrange("p a l -> p (a l)"),
                                          ps[:, TURN_BANKS[(2 * g + 1) % 4], :].bitcast(BF16)).then_inc(q1T_ready, 1)

            def row_max(a, p, units, banks=S_BANKS):
                for u in units:
                    n, head, o = p * UNITS + u, 2 * p + u % 2, 0
                    dve.wait_ge(score_made, a * HP * UNITS + n + 1)
                    for t in MAX_UNITS[u // 2]:
                        keys = P * (t + 1)
                        ins = nc.vector.tensor_reduce(row_maxima[:, t, head:head + 1],
                                                      ps[:, banks[n % 2], o:o + keys], AX.X, ALU.max)
                        o += keys
                    ins.then_inc(max_ready, 1)

            def split_max(a, p):
                heads = slice(2 * p, 2 * p + 2)
                dve.wait_ge(max_ready, (a * HP + p + 1) * UNITS)
                core_link(a, nc.vector.tensor_copy(qk_tok[:, 0, :, heads, MAX_AT], row_maxima[:, :, heads]))
                core_link(a, nc.vector.tensor_tensor(max_rest[:], row_maxima[:, :, heads],
                                                     qk_tok[:, 0, :, heads, MAX_AT], ALU.subtract))
                nc.vector.tensor_copy(qk_tok[:, 0, :, heads, MAX_AT + 1], max_rest[:]).then_inc(max_split, 1)

            def divide(a, g, banks=WEIGHED_BANKS):
                dve.wait_ge(weighedT_made, a * G + g + 1)
                sums = ps[:, banks[g % len(banks)], :].rearrange("p (t h w) -> p t h w", t=TT, h=Q)
                core_link(a, nc.vector.reciprocal(rec[:], sums[:, :, :, HD]))
                nc.vector.tensor_tensor(att[:, :, Q * g * HD:Q * (g + 1) * HD].rearrange("p t (h d) -> p t h d", h=Q),
                                        sums[:, :, :, 0:HD], rec[:].unsqueeze(3).broadcast_to([P, TT, Q, HD]),
                                        ALU.mult).then_inc(att_ready, 1)

            def attention_post(a):
                dve.wait_ge(bias_added, a + 1)
                dve.wait_ge(wo_made, a + 1)
                core_link(a, nc.vector.tensor_tensor(x[:].rearrange("p t d -> p (t d)"), ps[:, 5, :],
                                                     xin[:].rearrange("p t d -> p (t d)"), ALU.add))
                core_link.end()
                nc.vector.tensor_copy(spacer[:], x[:, 0, 0:1]).then_inc(xin_free, 1)

            def ffn(b, r, n, a=None, pre_n=None):
                f = b * FFNS + r
                norm_stats(n, x, ffn_link, f)
                norm_apply(n, x, xn)
                soft = a is not None and r == 1
                if soft:
                    row_max(a, 0, (2,), S_BANKS_FIRST)
                dve.wait_ge(xnT_ready, n + 1)
                ffn_link(f, nc.vector.tensor_scalar(x16[:, 0, :], xnT[:], X_SCALE, None, ALU.mult))
                nc.vector.scalar_tensor_tensor(x16[:, 1, :], xnT[:], X_SCALE, x16[:, 0, :], ALU.mult,
                                               ALU.subtract).then_inc(x16_ready, 1)
                if soft:
                    row_max(a, 0, (3,), S_BANKS_FIRST)
                dve.wait_ge(sig_ready, f + 1)
                nc.vector.memset(taken[:, :, 2:8], -1.0)
                for t in range(TT):
                    ins = nc.vector.max(best[:, t, :], score[:, t, :])
                ffn_link(f, ins)
                ffn_link(f, nc.vector.tensor_copy(taken[:, :, 0:2], best[:, :, 0:2]))
                nc.vector.memset(spacer[:], 0.0)
                for t in range(TT):
                    ins = nc.vector.match_replace(left[:, t, :], taken[:, t, :], score[:, t, :], 0.0)
                ffn_link(f, ins)
                nc.vector.tensor_tensor(route[:, :, 0:E], score[:, :, 0:E], left[:, :, 0:E],
                                        ALU.subtract).then_inc(route_ready, 1)
                dve.wait_ge(route_ready, f + 1)
                nc.vector.tensor_scalar(route_back[:], route[:], down_back[:], None, ALU.mult)
                if soft:
                    row_max(a, 0, (4, 5), S_BANKS_FIRST)
                    split_max(a, 0)

                def split_hidden(i, half):
                    two = slice(2 * half, 2 * half + 2)
                    src, high, low = hid[:, i % 2, two], hid16[:, i % 2, 0, two], hid16[:, i % 2, 1, two]
                    if i >= 2 and half == 0:
                        dve.wait_ge(down_made, f * X + i - 1)
                    if soft or i in (0, X - 1):
                        n = 2 * i + half if soft or i == 0 else 2 + half
                        dve.wait_ge(gelu_ready, f * X * C + i * C + 2 * half + 2)
                        nc.vector.tensor_scalar(high, src, hid_scale[:], None, ALU.mult).then_inc(own_high16_ready, 1)
                        dve.wait_ge(own_high16_ready, b * (4 + 2 * X) + r * 4 + n + 1)
                    else:
                        dve.wait_ge(high16_ready, (b + r) * 2 * (X - 2) + 2 * (i - 1) + half + 1)
                    nc.vector.scalar_tensor_tensor(low, src, hid_scale[:], high, ALU.mult,
                                                   ALU.subtract).then_inc(hid16_ready, 1)

                def combine(i):
                    dve.wait_ge(down_made, f * X + i + 1)
                    if i >= 2:
                        dve.wait_ge(sum_ready, f * X + i - 1)
                    bank = DOWN_BANKS[0 if soft else i % 2]
                    nc.vector.tensor_tensor(weighted[:, i % 2], ps[:, bank, :].rearrange("p (t d) -> p t d", t=TT),
                                            route_back[:, :, ORDER[i]:ORDER[i] + 1].broadcast_to([P, TT, D]),
                                            ALU.mult).then_inc(down_read, 1)

                x_flat = x[:].rearrange("p t d -> p (t d)")

                def pre_piece(n):
                    if n == 2:
                        norm_apply(pre_n, xin, xn_a)
                    if n in (6, 7):
                        rotate(a, 2 * (n - 6))
                        rotate(a, 2 * (n - 6) + 1)
                    for m, piece in ((8, rotated), (9, take_high), (10, less_high), (11, take_middle),
                                     (12, less_middle), (13, take_low)):
                        if n == m:
                            piece(a)
                    if n == 2 * HP - 1:
                        pre_queries(a, (0, 1))
                    if n == 2 * HP:
                        pre_queries(a, (2,))

                split_hidden(0, 0)
                split_hidden(0, 1)
                for i in range(X):
                    if i == (0 if soft else 1):
                        dve.wait_ge(base_made, f + 1)
                        nc.vector.tensor_tensor(x_flat, ps[:, MISC, :], x_flat, ALU.add).then_inc(base_added, 1)
                    maxima = soft and i + 1 < HP
                    if maxima:
                        row_max(a, i + 1, (0,))
                    if i + 1 < X:
                        split_hidden(i + 1, 0)
                    if a is not None and r == 0:
                        pre_piece(2 * i)
                    if maxima:
                        row_max(a, i + 1, (1,))
                    if soft and i in (2, 4, 6, 8):
                        divide(a, i // 2 - 1)
                    if maxima:
                        row_max(a, i + 1, (2,))
                    if i + 1 < X:
                        split_hidden(i + 1, 1)
                    if maxima:
                        row_max(a, i + 1, (3,))
                    combine(i)
                    if maxima:
                        row_max(a, i + 1, (4, 5))
                        split_max(a, i + 1)
                    if a is not None and r == 0:
                        pre_piece(2 * i + 1)
                        if i == 0:
                            dve.wait_ge(xin_ready, a * 16 + 16)
                            norm_stats(pre_n, xin, pre_link, a)
                dve.wait_ge(down_read, f * X + X)
                dve.wait_ge(sum_ready, f * X + X - 1)
                if r == 1:
                    dve.wait_ge(out_stored, b * 16 + 16)
                nc.vector.tensor_tensor((x, xout)[r][:], x[:], weighted[:, (X - 1) % 2],
                                        ALU.add).then_inc(sum_ready, 1)
                dve.wait_ge(sum_ready, f * X + X)
                ffn_link.end()

            def scan_block(b, n, a=None):
                norm_stats(n, x, scan_link, b)
                norm_apply(n, x, xn)
                if a is not None:
                    pre_queries(a, (3,))
                dve.wait_ge(step_ready, b + 1)
                nc.vector.tensor_scalar(decay, step, wa[:, 0:1], None, ALU.mult)
                scan_link(b, nc.vector.tensor_tensor(u_in, step, ps[0:N, 5, :], ALU.mult))
                nc.vector.tensor_tensor_scan(state, decay, u_in, 0.0, ALU.mult,
                                             ALU.add).then_inc(state_ready, 1)
                for c in range(2):
                    dve.wait_ge(centre_ready, b * 2 + c + 1)
                    ins = nc.vector.scalar_tensor_tensor(xcv[:, c, 1:L], ps[:, 1 + c, 0:L - 1], conv[:, c, 0:1],
                                                         xcv[:, c, 1:L], ALU.mult, ALU.add)
                scan_link(b, ins)
                for c in range(2):
                    ins = nc.vector.scalar_tensor_tensor(xcv[:, c, 0:L - 1], ps[:, 1 + c, 1:L], conv[:, c, 2:3],
                                                         xcv[:, c, 0:L - 1], ALU.mult, ALU.add)
                for c in range(2):
                    dve.wait_ge(y_made, b * 2 + c + 1)
                    dve.wait_ge(xs_ready, b * 2 + c + 1)
                    nc.vector.scalar_tensor_tensor(y[:, c, :], xs[:, c, :], dv[:, c:c + 1], ps[:, Y_BANKS[c], :],
                                                   ALU.mult, ALU.add).then_inc(y_ready, 1)
                dve.wait_ge(y_ready, b * 2 + 2)
                for c in range(2):
                    ins = nc.vector.tensor_tensor(diff[:, c, :], xcv[:, c, :], y[:, c, :], ALU.subtract)
                scan_link(b, ins)
                for c in range(2):
                    dve.wait_ge(gate_ready, b * 2 + c + 1)
                    scan_link(b, nc.vector.tensor_tensor(diff[:, c, :], diff[:, c, :], gate[:, c, :], ALU.mult))
                    nc.vector.tensor_tensor(z[:, c, :], diff[:, c, :], y[:, c, :], ALU.add).then_inc(z_ready, 1)
                if a is not None:
                    row_max(a, 0, (0, 1), S_BANKS_FIRST)
                dve.wait_ge(mo_made, b + 1)
                dve.wait_ge(residual_ready, b + 1)
                x_flat = x[:].rearrange("p t d -> p (t d)")
                scan_link(b, nc.vector.tensor_tensor(x_flat, ps[:, 1, :], x_flat, ALU.add))
                scan_link.end()

            steps = [0]

            def prep(ins):
                steps[0] += 1
                ins.then_inc(prep_step, 1)
                dve.wait_ge(prep_step, steps[0])

            def find_tops(k, piece):
                n = k * PIECES + piece
                nc.vector.tensor_reduce(tops_part[:, n:n + 1],
                                        piece_of((w1_raw, w2_raw)[k], piece), AX.X, ALU.max,
                                        apply_absolute_value=True).then_inc(tops_part_ready, 1)

            def join_tops():
                dve.wait_ge(tops_part_ready, 2 * PIECES)
                nc.vector.tensor_reduce(tops[:, 0:2], tops_part[:].rearrange("p (k n) -> p k n", k=2), AX.X, ALU.max)
                nc.vector.tensor_reduce(tops[:, 2:3], b1[:], AX.X, ALU.max,
                                        apply_absolute_value=True).then_inc(tops_found, 1)

            def take_low_weights(k, piece):
                raw, parts, scale = ((w1_raw, w1, up_scale), (w2_raw, w2, down_scale))[k]
                raw, high, low = (piece_of(t, piece) for t in (raw, parts[:, 0], parts[:, 1]))
                dve.wait_ge(high_ready, k * PIECES + piece + 1)
                nc.vector.scalar_tensor_tensor(low, raw, scale[:], high, ALU.mult,
                                               ALU.subtract).then_inc(low_ready, 1)

            def weight_pieces(i, which):
                for n in which:
                    if i < 4:
                        find_tops((4 * i + n) // PIECES, (4 * i + n) % PIECES)
                    if i >= 5:
                        take_low_weights((4 * (i - 5) + n) // PIECES, (4 * (i - 5) + n) % PIECES)

            def set_scales():
                dve.wait_ge(bounds_ready, 1)
                prep(nc.vector.scalar_tensor_tensor(bounds[:, 3:4], bounds[:, 0:1], float(D), bounds[:, 2:3],
                                                    ALU.mult, ALU.add))
                prep(nc.vector.tensor_scalar(bounds[:], bounds[:], TINY, None, ALU.max))
                prep(nc.vector.tensor_scalar(powers[:].bitcast(I32), bounds[:].bitcast(I32), EXPONENT, None,
                                             ALU.bitwise_and))
                prep(nc.vector.reciprocal(inverses[:], powers[:]))
                nc.vector.tensor_scalar(up_scale[:], inverses[:, 0:1], TOP, None, ALU.mult)
                nc.vector.tensor_scalar(down_scale[:], inverses[:, 1:2], TOP, None, ALU.mult)
                nc.vector.tensor_scalar(hid_scale[:], inverses[:, 3:4], TOP, None, ALU.mult)
                nc.vector.tensor_scalar(up_back[:], powers[:, 0:1], 1.0 / (TOP * X_SCALE), None, ALU.mult)
                prep(nc.vector.tensor_scalar(back_root[:], powers[:, 1:2], 1.0 / (TOP * TOP), None, ALU.mult))
                nc.vector.tensor_tensor(down_back[:], back_root[:], powers[:, 3:4], ALU.mult).then_inc(scales_ready, 1)

            dve.wait_ge(xin_ready, 16)
            norm_stats(0, xin, pre_link, 0)
            dve.wait_ge(ident_in, 16)
            nc.vector.tensor_copy(ident16[:], ident[:]).then_inc(ident16_ready, 1)
            norm_apply(0, xin, xn_a)
            dve.wait_ge(consts_in, 16 * len(attn_loads))
            dve.wait_ge(pads_set, KEY_PADS_SET)
            for t in range(TT):
                rotate(0, t)
            for piece in (rotated, take_high, less_high, take_middle, less_middle, take_low):
                piece(0)
            pre_queries(0)
            dve.wait_ge(ffn_in, 16 * len(ffn_loads))
            for i in range(HP + 1):
                if i == HP - 1:
                    dve.wait_ge(scan_in, 16 * len(scan_loads))
                    dve.wait_ge(pads_set, ALL_SET)
                    for c in range(2):
                        ins = nc.vector.tensor_scalar(step_inner[:, c, 0:N], bm[:, c, :], wdt[:, c:c + 1], None,
                                                      ALU.mult)
                    ins.then_inc(wb_ready, 1)
                for u in range(UNITS):
                    if i < HP:
                        row_max(0, i, (u,), S_BANKS_ALONE)
                    if u == UNITS - 1 and i < HP:
                        split_max(0, i)
                    if u == 3 and i in (3, 5, 7):
                        divide(0, i // 2 - 1, WEIGHED_ALONE)
                weight_pieces(i, (0, 1, 2, 3))
                if i == 3:
                    join_tops()
                if i == 4:
                    set_scales()
            divide(0, G - 1, WEIGHED_ALONE)
            attention_post(0)
            dve.wait_ge(pads_set, ALL_SET)
            dve.wait_ge(wa_ready, 1)
            dve.wait_ge(scales_ready, 1)
            with dve.Fori(0, B - 1) as b:
                ffn(b, 0, 4 * b + 1, b + 1, 4 * b + 2)
                scan_block(b, 4 * b + 3, b + 1)
                ffn(b, 1, 4 * b + 4, b + 1)
                attention_post(b + 1)
            last = B - 1
            ffn(last, 0, 4 * last + 1)
            scan_block(last, 4 * last + 2)
            ffn(last, 1, 4 * last + 3)


def shape_constants():
    exponents = np.arange(0, HD, 2, dtype=np.float32) / np.float32(HD)
    inv_freq = (1.0 / np.float32(10000.0) ** exponents).astype(np.float32)
    ang = np.arange(L, dtype=np.float32)[:, None] * inv_freq[None, :]
    cos = np.repeat(np.cos(ang), 2, axis=-1)
    sin = np.repeat(np.sin(ang), 2, axis=-1) * np.where(np.arange(HD) % 2 == 0, -1.0, 1.0)
    scale = np.array([1.0 / HD, 1.0])[:, None]

    def table(a):
        a = np.broadcast_to(a.reshape(TT, P, 1, HD), (TT, P, 2, HD)) * scale
        return a.transpose(1, 0, 2, 3).astype(np.float32)

    bf = mybir.dt.np(BF16)
    later = np.arange(P)[None, :] > np.arange(P)[:, None]
    return {
        "cos": table(cos), "sin": table(sin), "ident": np.eye(P, dtype=np.float32),
        "neg_eye": (NEG_ROOT * np.eye(P)).astype(bf),
        "mask_qk": (-NEG_ROOT * later).astype(bf), "mask_kq": (-NEG_ROOT * later.T).astype(bf),
    }


def kernel(**inputs):
    import concourse.bacc as bacc
    from concourse.bass_utils import run_bass_kernel_spmd

    a = {k: np.asarray(v) for k, v in inputs.items()}
    w1 = np.concatenate([a["L0_ffn_W1"], a["L0_ffn_Ws1"][None]], 0)
    w2 = np.concatenate([a["L0_ffn_W2"], a["L0_ffn_Ws2"][None]], 0)
    b1 = np.concatenate([a["L0_ffn_b1"], a["L0_ffn_bs1"][None]], 0)
    b2 = np.concatenate([a["L0_ffn_b2"], a["L0_ffn_bs2"][None]], 0)
    arrays = {
        "x": a["L0_attn_a_x"],
        "wqkv": np.concatenate([a["L0_attn_a_Wq"].T, a["L0_attn_a_Wk"].T, a["L0_attn_a_Wv"].T], 1),
        "wo": a["L0_attn_a_Wo"].T,
        "bo": a["L0_attn_a_bo"][None],
        "w1": w1.transpose(2, 0, 1),
        "b1": b1.reshape(X * C, P).T,
        "w2": w2.reshape(X, D, C, P).transpose(3, 0, 2, 1),
        "b2": b2,
        "wg": a["L0_ffn_Wg"].T,
        "gate_rows": np.repeat(np.stack([a["L0_ffn_bg"], a["L0_ffn_bias"]])[:, None], TT, 1),
        "a_mat": a["L0_attn_b_A"].reshape(2, P, N).transpose(1, 0, 2),
        "bm": a["L0_attn_b_Bm"].reshape(2, P, N).transpose(1, 0, 2),
        "cm": a["L0_attn_b_Cm"],
        "dv": a["L0_attn_b_Dv"].reshape(2, P).T,
        "wdt": a["L0_attn_b_W_dt"].reshape(2, P).T,
        "conv": a["L0_attn_b_conv_w"].reshape(2, P, K).transpose(1, 0, 2),
        "win": a["L0_attn_b_W_in"].T,
        "win_rows": a["L0_attn_b_W_in"][ED:].reshape(2, P, D).transpose(1, 0, 2),
        "wout": a["L0_attn_b_W_out"].T.reshape(2, P, D).transpose(1, 0, 2),
        **shape_constants(),
    }
    nc = bacc.Bacc("TRN2", target_bir_lowering=False, num_devices=1)
    args, given = [], {}
    for name, v in arrays.items():
        v = np.ascontiguousarray(v)
        given[f"in_{name}"] = v
        args.append(nc.dram_tensor(f"in_{name}", v.shape, mybir.dt.from_np(v.dtype), kind="ExternalInput").ap())
    out = nc.dram_tensor("out_x", (B, L, D), F32, kind="ExternalOutput").ap()
    hybrid_block_kernel(nc, *args, out)
    r = run_bass_kernel_spmd(nc, [given], core_ids=[0])
    return r.results[0]["out_x"]
```
